# Optimizing a Trainium2 kernel written in Bass

```python
import numpy as np
import jax
import jax.numpy as jnp

def _softmax(x, axis=-1):
    return jax.nn.softmax(x, axis=axis)

def _gelu(x):
    return jax.nn.gelu(x, approximate=True)

def _silu(x):
    return jax.nn.silu(x)

def _sigmoid(x):
    return jax.nn.sigmoid(x)

def _layernorm(x, axis=-1, eps=1e-05):
    m = jnp.mean(x, axis=axis, keepdims=True)
    v = jnp.var(x, axis=axis, keepdims=True)
    return (x - m) / jnp.sqrt(v + eps)

def _scatter_add(tgt, idx, src, axis=0):
    return tgt.at[idx].add(src)

def _segment_sum(src, seg, n):
    return jax.ops.segment_sum(src, seg, n)
kernel_name = 'mk_vit_tower_postln_d1_tok_img768_r4_0e045a'

def setup_inputs(seed: int=0):
    np.random.seed(seed)
    _w = jnp.asarray

    def _rec_inputs():
        import jax
        import jax.numpy as jnp
        _rk = jax.random.key(seed)
        x = -0.00016672 + 0.999947 * jax.random.normal(jax.random.fold_in(_rk, 1), (64, 3, 224, 224), jnp.float32)
        return x
    x = _rec_inputs()

    def _L0_tok_setup():
        import jax, jax.numpy as jnp
        import numpy as np
        CHANNEL = 3
        PATCH = 16
        D_MODEL = 192
        key = jax.random.key(seed)
        kx, kw = jax.random.split(key)
        x = jax.random.normal(kx, (64, CHANNEL, 96, 96), dtype=jnp.float32)
        fan_in = PATCH * PATCH * CHANNEL
        bound = 1.0 / np.sqrt(fan_in)
        W = jax.random.uniform(kw, (D_MODEL, fan_in), dtype=jnp.float32, minval=-bound, maxval=bound)
        return {'x': x, 'W': W}
    _L0_tok_all = _L0_tok_setup()
    _L0_tok_in = {k: v for k, v in _L0_tok_all.items() if k in ('W',)}
    del _L0_tok_all

    def _L0_attn_setup():
        import jax, jax.numpy as jnp
        import numpy as np
        B, N, E, H = (2, 512, 192, 12)
        D = E // H
        G = 16
        LN_EPS = 1e-05

        def _layernorm(x, w, b):
            mu = jnp.mean(x, axis=-1, keepdims=True)
            var = jnp.mean(jnp.square(x - mu), axis=-1, keepdims=True)
            return (x - mu) * jax.lax.rsqrt(var + LN_EPS) * w + b
        key = jax.random.key(seed)
        ks = jax.random.split(key, 8)
        s = E ** (-0.5)
        x = jax.random.normal(ks[0], (B, N, E), jnp.float32)
        log_slope = -2.0 ** (-8.0 * (jnp.arange(H, dtype=jnp.float32) + 1.0) / H)
        Wq = jax.random.normal(ks[1], (E, E), jnp.float32) * s
        Wk = jax.random.normal(ks[2], (E, E), jnp.float32) * s
        Wv = jax.random.normal(ks[3], (E, E), jnp.float32) * s
        Wo = jax.random.normal(ks[4], (E, E), jnp.float32) * s
        Wg1 = jax.random.normal(ks[5], (E, G), jnp.float32) * s
        Wg2 = jax.random.normal(ks[6], (G, E), jnp.float32) * G ** (-0.5)
        ln_w = jnp.ones((E,), jnp.float32)
        ln_b = jnp.zeros((E,), jnp.float32)
        return {'x': x, 'log_slope': log_slope, 'Wq': Wq, 'Wk': Wk, 'Wv': Wv, 'Wo': Wo, 'Wg1': Wg1, 'Wg2': Wg2, 'ln_w': ln_w, 'ln_b': ln_b}
    _L0_attn_all = _L0_attn_setup()
    _L0_attn_in = {k: v for k, v in _L0_attn_all.items() if k in ('log_slope', 'Wq', 'Wk', 'Wv', 'Wo', 'Wg1', 'Wg2', 'ln_w', 'ln_b')}
    del _L0_attn_all

    def _L0_ffn_setup():
        import jax, jax.numpy as jnp
        import numpy as np
        EPS_NORM = 1e-05
        RMS_EPS = 1e-05

        def _l2_normalize(v):
            n = jnp.sqrt(jnp.sum(v * v, axis=-1, keepdims=True))
            return v / jnp.maximum(n, EPS_NORM)

        def _rms_norm(x, weight, eps):
            ms = jnp.mean(x * x, axis=-1, keepdims=True)
            return x * jax.lax.rsqrt(ms + eps) * weight
        key = jax.random.key(seed)
        ks = jax.random.split(key, 6)
        B, T, D = (8, 1024, 192)
        S, F = (64, 768)
        x = jax.random.normal(ks[0], (B, T, D), dtype=jnp.float32)
        slots = 0.02 * jax.random.normal(ks[1], (S, D), dtype=jnp.float32)
        scale = jnp.ones((S,), dtype=jnp.float32)
        fc1_weight = 0.02 * jax.random.normal(ks[2], (S, D, F), dtype=jnp.float32)
        fc1_bias = jnp.zeros((S, F), dtype=jnp.float32)
        fc2_weight = 0.02 * jax.random.normal(ks[3], (S, F, D), dtype=jnp.float32)
        fc2_bias = jnp.zeros((S, D), dtype=jnp.float32)
        norm_weight = jnp.ones((D,), dtype=jnp.float32)
        return {'x': x, 'slots': slots, 'scale': scale, 'fc1_weight': fc1_weight, 'fc1_bias': fc1_bias, 'fc2_weight': fc2_weight, 'fc2_bias': fc2_bias, 'norm_weight': norm_weight}
    _L0_ffn_all = _L0_ffn_setup()
    _L0_ffn_in = {k: v for k, v in _L0_ffn_all.items() if k in ('slots', 'scale', 'fc1_weight', 'fc1_bias', 'fc2_weight', 'fc2_bias', 'norm_weight')}
    del _L0_ffn_all
    return {'x': x, 'L0_tok_W': _L0_tok_in['W'], 'L0_attn_log_slope': _L0_attn_in['log_slope'], 'L0_attn_Wq': _L0_attn_in['Wq'], 'L0_attn_Wk': _L0_attn_in['Wk'], 'L0_attn_Wv': _L0_attn_in['Wv'], 'L0_attn_Wo': _L0_attn_in['Wo'], 'L0_attn_Wg1': _L0_attn_in['Wg1'], 'L0_attn_Wg2': _L0_attn_in['Wg2'], 'L0_attn_ln_w': _L0_attn_in['ln_w'], 'L0_attn_ln_b': _L0_attn_in['ln_b'], 'L0_ffn_slots': _L0_ffn_in['slots'], 'L0_ffn_scale': _L0_ffn_in['scale'], 'L0_ffn_fc1_weight': _L0_ffn_in['fc1_weight'], 'L0_ffn_fc1_bias': _L0_ffn_in['fc1_bias'], 'L0_ffn_fc2_weight': _L0_ffn_in['fc2_weight'], 'L0_ffn_fc2_bias': _L0_ffn_in['fc2_bias'], 'L0_ffn_norm_weight': _L0_ffn_in['norm_weight']}

def reference(x, L0_tok_W, L0_attn_log_slope, L0_attn_Wq, L0_attn_Wk, L0_attn_Wv, L0_attn_Wo, L0_attn_Wg1, L0_attn_Wg2, L0_attn_ln_w, L0_attn_ln_b, L0_ffn_slots, L0_ffn_scale, L0_ffn_fc1_weight, L0_ffn_fc1_bias, L0_ffn_fc2_weight, L0_ffn_fc2_bias, L0_ffn_norm_weight):
    import jax
    import jax.numpy as jnp

    def _L0_tok_ref(x, W):
        import jax, jax.numpy as jnp
        import numpy as np
        CHANNEL = 3
        PATCH = 16
        D_MODEL = 192
        B, C, H, Wd = x.shape
        p = PATCH
        nH, nW = (H // p, Wd // p)
        patches = x.reshape(B, C, nH, p, nW, p)
        patches = patches.transpose(0, 2, 4, 3, 5, 1)
        flat = patches.reshape(B, nH * nW, p * p * C)
        return jnp.einsum('bnk,dk->bnd', flat, W)

    def _L0_attn_ref(x, log_slope, Wq, Wk, Wv, Wo, Wg1, Wg2, ln_w, ln_b):
        import jax, jax.numpy as jnp
        import numpy as np
        B, N, E, H = (2, 512, 192, 12)
        D = E // H
        G = 16
        LN_EPS = 1e-05

        def _layernorm(x, w, b):
            mu = jnp.mean(x, axis=-1, keepdims=True)
            var = jnp.mean(jnp.square(x - mu), axis=-1, keepdims=True)
            return (x - mu) * jax.lax.rsqrt(var + LN_EPS) * w + b
        b, n, e = x.shape
        h = log_slope.shape[0]
        d = e // h
        silu = jax.nn.silu
        q = silu(x @ Wq).reshape(b, n, h, d).transpose(0, 2, 1, 3)
        k = silu(x @ Wk).reshape(b, n, h, d).transpose(0, 2, 1, 3)
        v = silu(x @ Wv).reshape(b, n, h, d).transpose(0, 2, 1, 3)
        idx = jnp.arange(n, dtype=jnp.float32)
        diff = idx[:, None] - idx[None, :]
        keep = diff >= 0
        decay = jnp.where(keep, jnp.exp(log_slope[:, None, None] * jnp.maximum(diff, 0.0)), 0.0)
        energy = jnp.einsum('bhnd,bhmd->bhnm', q, k) * decay
        out = jnp.einsum('bhnm,bhmd->bhnd', energy, v)
        out = out.transpose(0, 2, 1, 3).reshape(b, n, e)
        gate = jax.nn.sigmoid(x @ Wg1 @ Wg2)
        out = out * gate
        out = out @ Wo
        out = _layernorm(out, ln_w, ln_b)
        return out

    def _L0_ffn_ref(x, slots, scale, fc1_weight, fc1_bias, fc2_weight, fc2_bias, norm_weight):
        import jax, jax.numpy as jnp
        import numpy as np
        EPS_NORM = 1e-05
        RMS_EPS = 1e-05

        def _l2_normalize(v):
            n = jnp.sqrt(jnp.sum(v * v, axis=-1, keepdims=True))
            return v / jnp.maximum(n, EPS_NORM)

        def _rms_norm(x, weight, eps):
            ms = jnp.mean(x * x, axis=-1, keepdims=True)
            return x * jax.lax.rsqrt(ms + eps) * weight
        xn = _rms_norm(x, norm_weight, RMS_EPS)
        tok = _l2_normalize(xn)
        sl = _l2_normalize(slots) * scale[:, None]
        logits = jnp.einsum('sd,btd->bst', sl, tok)
        dispatch_w = jax.nn.softmax(logits, axis=-1)
        combine_w = jax.nn.softmax(logits, axis=-2)
        y = jnp.einsum('btd,bst->bsd', xn, dispatch_w)
        y = jnp.einsum('sio,bsi->bso', fc1_weight, y) + fc1_bias
        y = jax.nn.gelu(y, approximate=False)
        y = jnp.einsum('sio,bsi->bso', fc2_weight, y) + fc2_bias
        out = jnp.einsum('bsd,bst->btd', y, combine_w)
        return out
    h = _L0_tok_ref(x, L0_tok_W)
    h = _layernorm(h + _L0_attn_ref(h, L0_attn_log_slope, L0_attn_Wq, L0_attn_Wk, L0_attn_Wv, L0_attn_Wo, L0_attn_Wg1, L0_attn_Wg2, L0_attn_ln_w, L0_attn_ln_b), axis=-1)
    h = _layernorm(h + _L0_ffn_ref(h, L0_ffn_slots, L0_ffn_scale, L0_ffn_fc1_weight, L0_ffn_fc1_bias, L0_ffn_fc2_weight, L0_ffn_fc2_bias, L0_ffn_norm_weight), axis=-1)
    return h

_drawn_inputs = setup_inputs


def setup_inputs(seed=0):
    import zlib

    import numpy as np

    out = dict(_drawn_inputs(seed))
    spreads = {'L0_attn_ln_w': (1.0, 0.2),
     'L0_attn_ln_b': (0.0, 0.1),
     'L0_ffn_scale': (1.0, 0.6),
     'L0_ffn_fc1_bias': (0.0, 0.8),
     'L0_ffn_fc2_bias': (0.0, 0.698),
     'L0_ffn_norm_weight': (1.0, 0.6)}
    factors = {'L0_ffn_slots': 8.0, 'L0_ffn_fc1_weight': 8.0, 'L0_ffn_fc2_weight': 8.0}
    for name, (base, spread) in spreads.items():
        noise = np.random.default_rng([zlib.crc32(name.encode()), seed]).standard_normal(out[name].shape)
        drawn = base * np.exp(spread * noise) if base else spread * noise
        out[name] = jnp.asarray(drawn.astype(out[name].dtype))
    for name, factor in factors.items():
        out[name] = (out[name] * factor).astype(out[name].dtype)
    return out
```

```python
from contextlib import ExitStack

import concourse.bass as bass
from concourse import mybir

F32 = mybir.dt.float32
ALU = mybir.AluOpType
ACT = mybir.ActivationFunctionType
AX = mybir.AxisListType.X

NB, C_IN, IMG, PATCH = 64, 3, 224, 16
GRID = IMG // PATCH
TOK = GRID * GRID
T = TOK // 2
PT = 2 * TOK
NP = NB // 2
D = 192
KP = PATCH * PATCH * C_IN // 128
G = D // 2
H = 12
HD = D // H
HG = H // 2
S = 64
F = 768
FH = F // 2
FJ = F // 128
NU = S // 2
RING = 4
TURNS = NU // RING
BANK = 512
EPS = 1e-5
ORDER = [(0, 0), (0, 1), (1, 0), (1, 1)]
UNIT = [(0, 2, 0, 0, TOK), (2, 2, 0, 0, TOK), (4, 2, 0, 0, TOK), (0, 3, 1, T, T), (3, 3, 1, T, T)]
UNITS = len(UNIT)
SC_BANKS = 3


def vit_tower(nc, xT, W, Wqkv, Wo, Wg1T, Wg2, log_slope, ln_w, ln_b, slots, scale, fc1, fc1b, fc2, fc2b,
              norm_w, out):
    h2_dram = nc.dram_tensor("h2_dram", [NP, T, 4, D], F32, kind="Internal").ap()
    comb_dram = nc.dram_tensor("comb_dram", [NP, 128, TOK], F32, kind="Internal").ap()
    y2_dram = nc.dram_tensor("y2_dram", [S, 2, NP, D], F32, kind="Internal").ap()
    y2_rows = y2_dram.rearrange("(u s) a p d -> u (s a p) d", s=2)
    y2_cols = y2_dram.rearrange("s a p d -> p a s d")
    out_v = out.rearrange("(p a) (c m) d -> p a m c d", a=2, c=2)
    with ExitStack() as ctx:
        def sb(name, shape):
            return ctx.enter_context(nc.sbuf_tensor(name, shape, F32))

        def sem(name):
            return ctx.enter_context(nc.semaphore(name))

        ps = ctx.enter_context(nc.psum_tensor("ps", [128, 8, BANK], F32))

        yT = sb("yT", [G + 1, 2, S, NB])
        ident = sb("ident", [128, 128])
        b2 = sb("b2", [128, D])
        WBUF = 2 * 2 * F + 2 * FJ * D
        early = sb("early", [128, 3 * WBUF + 3392])

        def taker(arena):
            at = [0]

            def take(*shape, skip=0):
                at[0] += skip
                n = 1
                for k in shape:
                    n *= k
                v = arena[:, at[0]:at[0] + n]
                at[0] += n
                assert at[0] <= arena.shape[1], at
                names = "abcd"[:len(shape)]
                if len(shape) == 1:
                    return v
                return v.rearrange(f"p ({' '.join(names)}) -> p {' '.join(names)}",
                                   **{k: n for k, n in zip(names[1:], shape[1:])})
            return take

        take = taker(early)
        x_sb = take(KP, PT)
        qm = take(2, HG, PT)
        p_sb = take(2, UNITS, PT)
        kT = take(2, PT)
        vpad = take(4, H * 32)
        w_sb = take(KP, D)
        wqkv = take(3, 2, D)
        dec = take(H, TOK)
        hT = take(2, PT)
        gt = take(2, PT)
        late = sb("late", [128, 6176])
        take = taker(late)
        og = take(2, PT)
        hb = take(4, D)
        t2 = take(4, D)
        h2 = take(4, D)
        xn = take(4, D)
        tok = take(4, D)
        tokT = take(2, PT)
        wo = take(2, D)
        wg = take(2, D)
        slT = sb("slT", [G, 2, S])
        mask = sb("mask", [G, HG])
        slope = sb("slope", [T, H])
        lnw, lnb, nw = sb("lnw", [T, D]), sb("lnb", [T, D]), sb("nw", [T, D])
        wg1, wg2 = sb("wg1", [16, D]), sb("wg2", [16, D])
        sl, slq, slst = sb("sl", [S, D]), sb("slq", [S, D]), sb("slst", [S, 4])
        st1, mv1 = sb("st1", [T, 4, 6]), sb("mv1", [T, 4, 2])
        st2, mv2 = sb("st2", [T, 4, 6]), sb("mv2", [T, 4, 2])
        rstd1, rstd2, rr, ms = (sb(n, [T, 4]) for n in ("rstd1", "rstd2", "rr", "ms"))
        ss, nrm, invn = (sb(n, [T, 4]) for n in ("ss", "nrm", "invn"))
        expo = sb("expo", [128, 4, 4])
        ve = sb("ve", [128, 5, 4])
        Ls, Es, Dn = sb("Ls", [128, TOK]), sb("Es", [128, TOK]), sb("Dn", [128, TOK])
        dist = Es[0:T, :]
        lmx, lneg, lsum, lrec = (sb(n, [128, 1]) for n in ("lmx", "lneg", "lsum", "lrec"))
        DT = sb("DT", [T, 2, 128])
        Lc, Ec, Cn = (sb(n, [T, 4, S]) for n in ("Lc", "Ec", "Cn"))
        cmx, csum, crec = (sb(n, [T, 4]) for n in ("cmx", "csum", "crec"))
        ysb = sb("ysb", [128, D])
        cst = sb("cst", [128, TOK])
        wbuf0 = sb("wbuf0", [128, WBUF])
        wbufs = [wbuf0[:, :]] + [early[:, n * WBUF:(n + 1) * WBUF] for n in range(3)]
        w1v = [w[:, 0:4 * F].rearrange("p (s k f) -> p s k f", s=2, k=2) for w in wbufs]
        w2v = [w[:, 4 * F:].rearrange("p (s j d) -> p s j d", s=2, j=FJ) for w in wbufs]
        take = taker(early)
        hg = take(F, skip=3 * WBUF)
        hgT = take(FJ, 128)
        y2st = take(2, D)
        ybuf = sb("ybuf", [G + 1, 2, 2, 2, NB])
        take = taker(late)
        h2r, res, o_sb = take(2, 4, D), take(2, 4, D), take(2, 4, D)
        cbuf = sb("cbuf", [128, 2, TOK])
        y2r, y2b = sb("y2r", [128, 2, D]), sb("y2b", [128, 2, D])
        st3, mv3 = sb("st3", [T, 2, 4, 6]), sb("mv3", [T, 2, 4, 2])
        rstd3, nb3 = sb("rstd3", [T, 2, 4]), sb("nb3", [T, 2, 4])

        loaded, ident_st, mask_st, dist_st = sem("loaded"), sem("ident_st"), sem("mask_st"), sem("dist_st")
        expo_st = sem("expo_st")
        zeroed, dec_exp, dec_rdy = sem("zeroed"), sem("dec_exp"), sem("dec_rdy")
        wg_mm, wg_sb, wo_halved = sem("wg_mm"), sem("wg_sb"), sem("wo_halved")
        sl_st, slT_mm, slT_sb = sem("sl_st"), sem("slT_mm"), sem("slT_sb")
        x_loaded = sem("x_loaded")
        hT_mm, hT_sb = sem("hT_mm"), sem("hT_sb")
        k_mm, k_sb = sem("k_mm"), sem("k_sb")
        g_mm, g_sb = sem("g_mm"), sem("g_sb")
        q_mm, qm_sb = sem("q_mm"), sem("qm_sb")
        v_mm, v_sb = sem("v_mm"), sem("v_sb")
        ht_mm, hb_sb = sem("ht_mm"), sem("hb_sb")
        sc_mm, p_rdy = sem("sc_mm"), sem("p_rdy")
        pv_mm, og_sb = sem("pv_mm"), sem("og_sb")
        wo_mm = sem("wo_mm")
        mv1_rdy, rstd1_rdy = sem("mv1_rdy"), sem("rstd1_rdy")
        t1_rdy, t2_rdy = sem("t1_rdy"), sem("t2_rdy")
        mv2_rdy, rstd2_rdy = sem("mv2_rdy"), sem("rstd2_rdy")
        ms_rdy, rr_rdy = sem("ms_rdy"), sem("rr_rdy")
        ve1_rdy, ve2_rdy, ve3_rdy, ve4_rdy = (sem(n) for n in ("ve1_rdy", "ve2_rdy", "ve3_rdy", "ve4_rdy"))
        h2_rdy, xn_rdy, ss_rdy = sem("h2_rdy"), sem("xn_rdy"), sem("ss_rdy")
        nrm_rdy, invn_rdy, tok_rdy = sem("nrm_rdy"), sem("invn_rdy"), sem("tok_rdy")
        h2_stored = sem("h2_stored")
        tokT_mm, tokT_sb = sem("tokT_mm"), sem("tokT_sb")
        lg_mm, Ls_rdy, lmx_rdy, lneg_rdy = (sem(n) for n in ("lg_mm", "Ls_rdy", "lmx_rdy", "lneg_rdy"))
        Es_rdy, lrec_rdy, Dn_rdy = sem("Es_rdy"), sem("lrec_rdy"), sem("Dn_rdy")
        lt_mm, cmx_rdy, Lc_rdy, Ec_rdy = (sem(n) for n in ("lt_mm", "cmx_rdy", "Lc_rdy", "Ec_rdy"))
        csum_rdy, crec_rdy, Cn_rdy = sem("csum_rdy"), sem("crec_rdy"), sem("Cn_rdy")
        dt_mm, DT_sb = sem("dt_mm"), sem("DT_sb")
        y_mm, y_sb, yT_mm, yT_sb = sem("y_mm"), sem("y_sb"), sem("yT_mm"), sem("yT_sb")
        cb_mm, cb_sb, comb_stored = sem("cb_mm"), sem("cb_sb"), sem("comb_stored")
        w_loaded = [sem(f"w_loaded{n}") for n in range(RING)]
        ybuf_rdy, fc1_mm, gelu_rdy = sem("ybuf_rdy"), sem("fc1_mm"), sem("gelu_rdy")
        tr_mm, hgT_rdy, fc2_mm, y2st_rdy = (sem(n) for n in ("tr_mm", "hgT_rdy", "fc2_mm", "y2st_rdy"))
        y2_stored = [sem("y2_stored0"), sem("y2_stored1")]
        h2r_loaded = [sem("h2r_loaded0"), sem("h2r_loaded1")]
        y2r_loaded = [sem("y2r_loaded0"), sem("y2r_loaded1")]
        cbuf_loaded = [sem("cbuf_loaded0"), sem("cbuf_loaded1")]
        y2b_rdy, cmb_mm, res_rdy = (sem(n) for n in ("y2b_rdy", "cmb_mm", "res_rdy"))
        mv3_rdy, rstd3_rdy = sem("mv3_rdy"), sem("rstd3_rdy")
        nb3_rdy, o_rdy = sem("nb3_rdy"), sem("o_rdy")
        out_stored = [sem("out_stored0"), sem("out_stored1")]

        def phase1(eng, step):
            step(0, True, False, False)
            step(1, True, True, False)
            with eng.Fori(2, NP) as i:
                step(i, True, True, True)
            step(NP, False, True, True)
            step(NP + 1, False, False, True)

        def phase2(eng, step):
            for n in range(RING):
                step(n, n, 0)
            with eng.Fori(1, TURNS) as v:
                for n in range(RING):
                    step(RING * v + n, n, v)

        def phase3(eng, step):
            for par in range(2):
                step(par, par, 0)
            with eng.Fori(1, NP // 2) as w:
                for par in range(2):
                    step(2 * w + par, par, w)

        def at_start(w):
            return isinstance(w, int) and w == 0

        block = ctx.enter_context(nc.Block())

        @block.sync
        def _(sp):
            loads = [
                (w_sb, W), (wqkv[0:G], Wqkv), (wo[0:G], Wo), (wg1[:, :], Wg1T), (wg2[:, :], Wg2),
                (slope[:, :], log_slope.partition_broadcast(T)), (lnw[:, :], ln_w.partition_broadcast(T)),
                (lnb[:, :], ln_b.partition_broadcast(T)), (nw[:, :], norm_w.partition_broadcast(T)),
                (sl[:, :], slots), (slst[:, 3:4], scale), (b2[0:S, :], fc2b), (b2[S:128, :], fc2b),
            ]
            assert len(loads) == N_LOADS
            sp.dma_start(x_sb, xT[0]).then_inc(x_loaded, 16)
            for dst, src in loads:
                sp.dma_start(dst, src).then_inc(loaded, 16)

            def load_weights(u, n):
                sp.dma_start(w1v[n][0:G], fc1[u]).then_inc(w_loaded[n], 16)
                sp.dma_start(w1v[n][G:G + 1, :, 1, :], fc1b[u]).then_inc(w_loaded[n], 16)
                sp.dma_start(w2v[n], fc2[u]).then_inc(w_loaded[n], 16)

            load_weights(0, 0)

            def store_h2(j):
                sp.wait_ge(h2_rdy, 4 * j + 4)
                sp.dma_start(h2_dram[j], h2[0:T]).then_inc(h2_stored, 16)

            def store_comb(j):
                sp.wait_ge(cb_sb, j + 1)
                sp.dma_start(comb_dram[j], cst[:, :]).then_inc(comb_stored, 16)

            def step(i, c, tail):
                sp.wait_ge(hT_mm, 2 * i + 2)
                sp.dma_start(x_sb, xT[i + 1]).then_inc(x_loaded, 16)
                if tail:
                    store_comb(i - 2)
                if c:
                    store_h2(i - 1)

            step(0, False, False)
            step(1, True, False)
            with sp.Fori(2, NP - 1) as i:
                step(i, True, True)
            store_comb(NP - 3)
            store_h2(NP - 2)
            sp.wait_ge(pv_mm, 4 * NP)
            sp.wait_ge(og_sb, 2 * NP)
            for n in range(1, RING):
                load_weights(n, n)
            store_comb(NP - 2)
            store_h2(NP - 1)
            store_comb(NP - 1)

            def load_comb(p, par):
                sp.dma_start(cbuf[:, par], comb_dram[p]).then_inc(cbuf_loaded[par], 16)

            def load_h2(p, par):
                sp.dma_start(h2r[0:T, par], h2_dram[p]).then_inc(h2r_loaded[par], 16)

            def load_y2(p, par):
                for a in range(2):
                    sp.dma_start(y2r[64 * a:64 * a + 64, par, :], y2_cols[p, a]).then_inc(y2r_loaded[par], 16)

            def slot_step(u, n, more):
                sp.wait_ge(y2st_rdy, u + 1)
                sp.dma_start(y2_rows[u], y2st[:, n % 2, :]).then_inc(y2_stored[n % 2], 16)
                if more:
                    load_weights(u + RING, n)
            with sp.Fori(0, TURNS - 1) as v:
                for n in range(RING):
                    slot_step(RING * v + n, n, True)
            for n in range(RING):
                slot_step(RING * (TURNS - 1) + n, n, False)

            sp.wait_ge(h2_stored, 16 * NP)
            sp.wait_ge(comb_stored, 16 * NP)
            for par in range(2):
                load_comb(par, par)
                load_h2(par, par)
            for par in range(2):
                sp.wait_ge(y2_stored[par], 16 * NU // 2)
            for par in range(2):
                load_y2(par, par)

            def store_out(p, par):
                sp.wait_ge(o_rdy, 4 * p + 4)
                for a in range(2):
                    sp.dma_start(out_v[p, a], o_sb[0:T, par, 2 * a:2 * a + 2]).then_inc(out_stored[par], 16)
            with sp.Fori(0, NP // 2 - 1) as w:
                for par in range(2):
                    p = 2 * w + par
                    sp.wait_ge(y2b_rdy, p + 1)
                    load_y2(p + 2, par)
                    sp.wait_ge(cmb_mm, p + 1)
                    load_comb(p + 2, par)
                    sp.wait_ge(res_rdy, p + 1)
                    load_h2(p + 2, par)
                    store_out(p, par)
            for par in range(2):
                store_out(NP - 2 + par, par)
            for par in range(2):
                sp.wait_ge(out_stored[par], 32 * (NP // 2))

        @block.gpsimd
        def _(pool):
            pool.iota(dist, [[1, TOK]], base=0, channel_multiplier=-1,
                      allow_small_or_imprecise_dtypes=True).then_inc(dist_st, 1)
            pool.wait_ge(ident_st, 1)
            pool.affine_select(out=ident[:, :], in_=ident[:, :], compare_op=ALU.not_equal, fill=1.0, base=0,
                               pattern=[[-1, 128]], channel_multiplier=1).then_inc(ident_st, 1)
            pool.wait_ge(mask_st, 1)
            pool.affine_select(out=mask[:, :], in_=mask[:, :], compare_op=ALU.is_ge, fill=0.0, base=0,
                               pattern=[[-HD, HG]], channel_multiplier=1).then_inc(mask_st, 1)
            pool.wait_ge(mask_st, 2)
            pool.affine_select(out=mask[:, :], in_=mask[:, :], compare_op=ALU.is_ge, fill=0.0, base=HD - 1,
                               pattern=[[HD, HG]], channel_multiplier=-1).then_inc(mask_st, 1)
            pool.wait_ge(dist_st, 1)
            pool.tensor_scalar(dist, dist, 0.0, None, ALU.max).then_inc(dist_st, 1)
            pool.wait_ge(sl_st, 1)
            pool.wait_ge(expo_st, 4)
            pool.tensor_tensor(slst[:, 1:2], slst[:, 0:1], expo[0:S, 1, 0:1], ALU.pow).then_inc(sl_st, 1)
            pool.wait_ge(sl_st, 2)
            pool.tensor_scalar(slst[:, 1:2], slst[:, 1:2], EPS, None, ALU.max).then_inc(sl_st, 1)
            pool.wait_ge(dec_exp, H)
            pool.affine_select(out=dec[0:T], in_=dec[0:T], compare_op=ALU.is_ge, fill=0.0, base=0,
                               pattern=[[0, H], [1, TOK]], channel_multiplier=-1).then_inc(dec_rdy, 1)

            def step(i, has_a, c, tail):
                if not c:
                    return
                j = i - 1
                pool.wait_ge(mv1_rdy, 4 * j + 4)
                pool.tensor_tensor(ve[0:T, 0], mv1[:, :, 1], expo[0:T, 3], ALU.add).then_inc(ve1_rdy, 1)
                pool.wait_ge(ve1_rdy, j + 1)
                pool.tensor_tensor(rstd1[:, :], ve[0:T, 0], expo[0:T, 0], ALU.pow).then_inc(rstd1_rdy, 1)
                pool.wait_ge(mv2_rdy, 4 * j + 4)
                pool.tensor_tensor(ve[0:T, 1], mv2[:, :, 1], expo[0:T, 3], ALU.add).then_inc(ve2_rdy, 1)
                pool.wait_ge(ve2_rdy, j + 1)
                pool.tensor_tensor(rstd2[:, :], ve[0:T, 1], expo[0:T, 0], ALU.pow).then_inc(rstd2_rdy, 1)
                pool.wait_ge(rstd2_rdy, j + 1)
                pool.tensor_tensor(ms[:, :], mv2[:, :, 1], rstd2[:, :], ALU.mult).then_inc(ms_rdy, 1)
                pool.wait_ge(ms_rdy, 2 * j + 1)
                pool.tensor_tensor(ms[:, :], ms[:, :], rstd2[:, :], ALU.mult).then_inc(ms_rdy, 1)
                pool.wait_ge(ms_rdy, 2 * j + 2)
                pool.tensor_tensor(ve[0:T, 2], ms[:, :], expo[0:T, 3], ALU.add).then_inc(ve3_rdy, 1)
                pool.wait_ge(ve3_rdy, j + 1)
                pool.tensor_tensor(rr[:, :], ve[0:T, 2], expo[0:T, 0], ALU.pow).then_inc(rr_rdy, 1)
                pool.wait_ge(nrm_rdy, j + 1)
                pool.tensor_tensor(invn[:, :], nrm[:, :], expo[0:T, 0], ALU.pow).then_inc(invn_rdy, 1)
                pool.wait_ge(invn_rdy, j + 1)
                for t in range(4):
                    pool.tensor_tensor(tok[0:T, t], xn[0:T, t], invn[:, t:t + 1].to_broadcast([T, D]), ALU.mult)\
                        .then_inc(tok_rdy, 1)
                pool.wait_ge(lmx_rdy, j + 1)
                pool.tensor_tensor(lneg[:, :], lmx[:, :], expo[:, 2, 0:1], ALU.mult).then_inc(lneg_rdy, 1)
                pool.wait_ge(lrec_rdy, j + 1)
                pool.tensor_tensor(Dn[:, :], Es[:, :], lrec[:, 0:1].to_broadcast([128, TOK]), ALU.mult).then_inc(Dn_rdy, 1)
                pool.wait_ge(crec_rdy, j + 1)
                pool.tensor_tensor(Cn[:, :, :], Ec[:, :, :], crec[:, :].unsqueeze(2).to_broadcast([T, 4, S]),
                                   ALU.mult).then_inc(Cn_rdy, 1)
            phase1(pool, step)

            pool.wait_ge(yT_sb, 2 * NP)
            pool.wait_ge(zeroed, 2)

            def slot_step(u, n, v):
                if not (isinstance(u, int) and u < 2):
                    pool.wait_ge(fc1_mm, u - 1)
                src = yT[:, :, :, :].rearrange("p k (u s) b -> p k u s b", s=2)
                pool.tensor_copy(ybuf[:, n % 2], src[:, :, u]).then_inc(ybuf_rdy, 1)
            phase2(pool, slot_step)

            def bias(p, par, w):
                if not at_start(w):
                    pool.wait_ge(cmb_mm, p - 1)
                pool.wait_ge(y2r_loaded[par], 32 * w + 32)
                pool.tensor_tensor(y2b[:, par], y2r[:, par], b2[:, :], ALU.add).then_inc(y2b_rdy, 1)

            def out_rstd(p, par):
                pool.wait_ge(mv3_rdy, 4 * p + 4)
                pool.tensor_tensor(ve[0:T, 3 + par], mv3[:, par, :, 1], expo[0:T, 3], ALU.add).then_inc(ve4_rdy, 1)
                pool.wait_ge(ve4_rdy, p + 1)
                pool.tensor_tensor(rstd3[:, par], ve[0:T, 3 + par], expo[0:T, 0], ALU.pow).then_inc(rstd3_rdy, 1)

            def out_step(p, par, w):
                bias(p, par, w)
                if not (at_start(w) and par == 0):
                    out_rstd(p - 1, 1 - par)
            phase3(pool, out_step)
            out_rstd(NP - 1, 1)

        @block.scalar
        def _(act):
            act.wait_ge(loaded, 16 * N_LOADS)
            act.wait_ge(dist_st, 2)
            for h in range(H):
                act.activation(dec[0:T, h, :], dist, ACT.Exp, scale=slope[:, h:h + 1]).then_inc(dec_exp, 1)
            act.wait_ge(mask_st, 3)
            act.wait_ge(zeroed, 2)

            def step(i, has_a, c, tail):
                j = i - 1
                if has_a:
                    for g in range(2):
                        act.wait_ge(hT_mm, 2 * i + g + 1)
                        act.activation(hT[0:G, g], ps[0:G, g, 0:PT], ACT.Copy).then_inc(hT_sb, 1)
                if tail:
                    act.wait_ge(yT_mm, i - 1)
                    for k in range(2):
                        dst = yT[0:G, k].rearrange("x s (a p) -> x a s p", a=2)[:, :, :, i - 2]
                        src = ps[0:G, 7, 128 * k:128 * k + 128].rearrange("x (a s) -> x a s", a=2)
                        act.activation(dst, src, ACT.Copy).then_inc(yT_sb, 1)
                    if not (isinstance(i, int) and i == 2):
                        act.wait_ge(comb_stored, 16 * (i - 2))
                    act.wait_ge(cb_mm, i - 1)
                    act.activation(cst[:, :], ps[:, 4, 0:TOK], ACT.Copy).then_inc(cb_sb, 1)
                if has_a:
                    for g in range(2):
                        act.wait_ge(k_mm, 2 * i + g + 1)
                        act.activation(kT[0:G, g], ps[0:G, g, 0:PT], ACT.Silu).then_inc(k_sb, 1)
                    if c:
                        act.wait_ge(og_sb, 2 * i)
                    for g in range(2):
                        act.wait_ge(g_mm, 2 * i + g + 1)
                        act.activation(gt[0:G, g], ps[0:G, g, 0:PT], ACT.Tanh, scale=0.5).then_inc(g_sb, 1)
                    for g in range(2):
                        act.wait_ge(q_mm, 2 * i + g + 1)
                        for m in range(HG):
                            last = act.activation(qm[0:G, g, m], ps[0:G, g, 0:PT], ACT.Silu,
                                                  scale=mask[:, m:m + 1])
                        last.then_inc(qm_sb, 1)
                        act.wait_ge(v_mm, 2 * i + g + 1)
                        dst = vpad[0:T, 2 * g:2 * g + 2].rearrange("p t (j q d) -> p (t j) q d", q=4, d=HD)
                        src = ps[0:T, 4 + 3 * g, 0:2 * D].rearrange("p (j q d) -> p j q d", q=2, d=HD)
                        act.activation(dst[:, :, 0:4:3, :], src, ACT.Silu).then_inc(v_sb, 1)
                if c:
                    act.wait_ge(tokT_mm, j + 1)
                    act.activation(tokT[0:G], ps[0:G, 0:2, 0:PT], ACT.Copy).then_inc(tokT_sb, 1)
                    act.wait_ge(lg_mm, j + 1)
                    act.activation(Ls[:, :], ps[:, 7, 0:TOK], ACT.Copy).then_inc(Ls_rdy, 1)
                    act.wait_ge(lneg_rdy, j + 1)
                    act.wait_ge(Ls_rdy, j + 1)
                    act.activation(Es[:, :], Ls[:, :], ACT.Exp, bias=lneg[:, 0:1], accum_out=lsum[:, 0:1])\
                        .then_inc(Es_rdy, 1)
                    act.wait_ge(Lc_rdy, j + 1)
                    act.activation(Ec[:, :, :], Lc[:, :, :], ACT.Exp).then_inc(Ec_rdy, 1)
                    act.wait_ge(dt_mm, j + 1)
                    act.activation(DT[:, :, :], ps[0:T, 1, 0:256].rearrange("p (c s) -> p c s", c=2),
                                   ACT.Copy).then_inc(DT_sb, 1)
                    act.wait_ge(y_mm, j + 1)
                    act.activation(ysb[:, :], ps[:, 7, 0:D], ACT.Copy).then_inc(y_sb, 1)
            phase1(act, step)

            def slot_step(u, n, v):
                act.wait_ge(fc1_mm, u + 1)
                act.activation(hg.rearrange("p (x f) -> p x f", x=2), ps[:, 0:2, 0:FH], ACT.Gelu)\
                    .then_inc(gelu_rdy, 1)
            phase2(act, slot_step)

            def out_step(p, par, w):
                act.wait_ge(nb3_rdy, p + 1)
                act.wait_ge(rstd3_rdy, p + 1)
                if not at_start(w):
                    act.wait_ge(out_stored[par], 32 * w)
                for t in range(4):
                    act.activation(o_sb[0:T, par, t], res[0:T, par, t], ACT.Identity,
                                   bias=nb3[:, par, t:t + 1], scale=rstd3[:, par, t:t + 1]).then_inc(o_rdy, 1)
            phase3(act, out_step)

        @block.vector
        def _(dve):
            dve.memset(ident[:, :], 0.0).then_inc(ident_st, 1)
            dve.memset(mask[:, :], 1.0).then_inc(mask_st, 1)
            for n, e in enumerate((-0.5, 0.5, -1.0, EPS)):
                dve.memset(expo[:, n], e).then_inc(expo_st, 1)
            dve.memset(vpad, 0.0).then_inc(zeroed, 1)
            dve.memset(yT[G:G + 1, :, :, :], 1.0).then_inc(zeroed, 1)
            dve.wait_ge(loaded, 16 * N_LOADS)
            dve.tensor_scalar(wo[0:G], wo[0:G], 0.5, None, ALU.mult).then_inc(wo_halved, 1)
            dve.tensor_tensor_reduce(out=slq[:, :], in0=sl[:, :], in1=sl[:, :], scale=1.0, scalar=0.0,
                                     op0=ALU.mult, op1=ALU.add, accum_out=slst[:, 0:1]).then_inc(sl_st, 1)
            dve.wait_ge(sl_st, 3)
            dve.reciprocal(slst[:, 2:3], slst[:, 1:2]).then_inc(sl_st, 1)
            dve.wait_ge(sl_st, 4)
            dve.tensor_scalar(slq[:, :], sl[:, :], slst[:, 2:3], slst[:, 3:4], ALU.mult, ALU.mult)\
                .then_inc(sl_st, 1)
            dve.wait_ge(wg_mm, 1)
            dve.tensor_copy(wg[0:G], ps[0:G, 0, 0:2 * D].rearrange("p (k d) -> p k d", k=2)).then_inc(wg_sb, 1)
            dve.wait_ge(slT_mm, 1)
            dve.tensor_copy(slT[:, :, :], ps[0:G, 1, 0:2 * S].rearrange("p (k s) -> p k s", k=2))\
                .then_inc(slT_sb, 1)
            dve.wait_ge(dec_rdy, 1)

            def norms(j):
                for t in range(4):
                    if t % 2 == 0:
                        dve.wait_ge(wo_mm, 2 * j + t // 2 + 1)
                    dve.bn_stats(st1[:, t, :], ps[0:T, 2 + t // 2, (t % 2) * D:(t % 2) * D + D])
                dve.drain()
                for t in range(4):
                    dve.bn_aggr(mv1[:, t, :], st1[:, t, :]).then_inc(mv1_rdy, 1)
                for t in range(4):
                    dve.wait_ge(mv1_rdy, 4 * j + t + 1)
                    dve.scalar_tensor_tensor(t2[0:T, t], ps[0:T, 2 + t // 2, (t % 2) * D:(t % 2) * D + D],
                                             mv1[:, t, 0:1], lnw[:, :], ALU.subtract, ALU.mult)\
                        .then_inc(t1_rdy, 1)
                dve.wait_ge(rstd1_rdy, j + 1)
                for t in range(4):
                    dve.wait_ge(t1_rdy, 4 * j + t + 1)
                    dve.scalar_tensor_tensor(t2[0:T, t], t2[0:T, t], rstd1[:, t:t + 1], hb[0:T, t],
                                             ALU.mult, ALU.add).then_inc(t2_rdy, 1)
                for t in range(4):
                    dve.wait_ge(t2_rdy, 4 * j + t + 1)
                    dve.bn_stats(st2[:, t, :], t2[0:T, t])
                dve.drain()
                for t in range(4):
                    dve.bn_aggr(mv2[:, t, :], st2[:, t, :]).then_inc(mv2_rdy, 1)
                dve.wait_ge(mv2_rdy, 4 * j + 4)
                dve.wait_ge(rstd2_rdy, j + 1)
                if not (isinstance(j, int) and j == 0):
                    dve.wait_ge(h2_stored, 16 * j)
                for t in range(4):
                    dve.tensor_scalar(h2[0:T, t], t2[0:T, t], mv2[:, t, 0:1], rstd2[:, t:t + 1],
                                      ALU.subtract, ALU.mult).then_inc(h2_rdy, 1)

            def slot_tokens(j, tail):
                dve.wait_ge(rr_rdy, j + 1)
                if tail:
                    dve.wait_ge(y_mm, j)
                for t in range(4):
                    dve.wait_ge(h2_rdy, 4 * j + t + 1)
                    dve.scalar_tensor_tensor(xn[0:T, t], h2[0:T, t], rr[:, t:t + 1], nw[:, :],
                                             ALU.mult, ALU.mult).then_inc(xn_rdy, 1)
                for t in range(4):
                    dve.wait_ge(xn_rdy, 4 * j + t + 1)
                    dve.tensor_tensor_reduce(out=tok[0:T, t], in0=xn[0:T, t], in1=xn[0:T, t], scale=1.0,
                                             scalar=0.0, op0=ALU.mult, op1=ALU.add,
                                             accum_out=ss[:, t:t + 1]).then_inc(ss_rdy, 1)
                dve.wait_ge(ss_rdy, 4 * j + 4)
                dve.tensor_scalar(nrm[:, :], ss[:, :], EPS * EPS, None, ALU.max).then_inc(nrm_rdy, 1)

            def decay(i, k):
                g, a = ORDER[k]
                if k < 2:
                    pass
                else:
                    dve.wait_ge(pv_mm, 4 * i + k - 1)
                for u, (h0, nh, _, n0, n) in enumerate(UNIT):
                    dve.wait_ge(sc_mm, 4 * UNITS * i + UNITS * k + u + 1)
                    src = ps[0:T, 2 + (UNITS * k + u) % SC_BANKS, 0:nh * n].rearrange("p (h n) -> p h n", h=nh)
                    dst = p_sb[0:T, k % 2, u, 0:nh * n].rearrange("p (h n) -> p h n", h=nh)
                    dve.tensor_tensor(dst, src, dec[0:T, g * HG + h0:g * HG + h0 + nh, 0:n], ALU.mult)\
                        .then_inc(p_rdy, 1)

            def step(i, has_a, c, tail):
                j = i - 1
                if c:
                    norms(j)
                if has_a:
                    for x in range(2):
                        dve.wait_ge(ht_mm, 2 * i + x + 1)
                        dve.tensor_tensor(hb[0:T, 2 * x:2 * x + 2],
                                          ps[0:T, 5 + x, 0:2 * D].rearrange("p (t d) -> p t d", t=2),
                                          lnb[:, :].unsqueeze(1).to_broadcast([T, 2, D]), ALU.add)\
                            .then_inc(hb_sb, 1)
                if c:
                    slot_tokens(j, tail)
                if has_a:
                    decay(i, 0)
                    decay(i, 1)
                if c:
                    dve.wait_ge(Ls_rdy, j + 1)
                    dve.reduce_max(lmx[:, :], Ls[:, :], AX).then_inc(lmx_rdy, 1)
                if has_a:
                    decay(i, 2)
                if c:
                    dve.wait_ge(Es_rdy, j + 1)
                    dve.reciprocal(lrec[:, :], lsum[:, :]).then_inc(lrec_rdy, 1)
                    dve.wait_ge(lt_mm, j + 1)
                    lt = ps[0:T, 0, 0:256].rearrange("p (x s) -> p x s", s=S)
                    dve.reduce_max(cmx[:, :], lt, AX).then_inc(cmx_rdy, 1)
                    dve.wait_ge(cmx_rdy, j + 1)
                    dve.tensor_tensor(Lc[:, :, :], lt, cmx[:, :].unsqueeze(2).to_broadcast([T, 4, S]),
                                      ALU.subtract).then_inc(Lc_rdy, 1)
                if has_a:
                    decay(i, 3)
                    for g in range(2):
                        dve.wait_ge(pv_mm, 4 * i + 2 * g + 2)
                        dve.wait_ge(g_sb, 2 * i + g + 1)
                        dve.scalar_tensor_tensor(og[0:G, g], gt[0:G, g], 1.0, ps[0:G, 5 + g, 0:PT],
                                                 ALU.add, ALU.mult).then_inc(og_sb, 1)
                if c:
                    dve.wait_ge(Ec_rdy, j + 1)
                    dve.reduce_sum(csum[:, :], Ec[:, :, :], AX).then_inc(csum_rdy, 1)
                    dve.wait_ge(csum_rdy, j + 1)
                    dve.reciprocal(crec[:, :], csum[:, :]).then_inc(crec_rdy, 1)
            phase1(dve, step)

            def slot_step(u, n, v):
                par = n % 2
                dve.wait_ge(tr_mm, u + 1)
                dve.tensor_copy(hgT.rearrange("p (x j) b -> p x (j b)", x=2), ps[:, 2:4, 0:FH])\
                    .then_inc(hgT_rdy, 1)
                if not (isinstance(u, int) and u < 2):
                    dve.wait_ge(y2_stored[par], 16 * (RING // 2 * v + n // 2))
                dve.wait_ge(fc2_mm, u + 1)
                dve.tensor_copy(y2st[:, par], ps[:, 4 + par, 0:D]).then_inc(y2st_rdy, 1)
            phase2(dve, slot_step)

            def out_step(p, par, w):
                dve.wait_ge(cmb_mm, p + 1)
                dve.wait_ge(h2r_loaded[par], 16 * w + 16)
                if not at_start(w):
                    dve.wait_ge(o_rdy, 4 * (p - 1))
                dve.tensor_tensor(res[0:T, par].rearrange("p (x t) d -> p x (t d)", x=2),
                                  ps[0:T, 2 * par:2 * par + 2, 0:2 * D],
                                  h2r[0:T, par].rearrange("p (x t) d -> p x (t d)", x=2), ALU.add)\
                    .then_inc(res_rdy, 1)
                dve.wait_ge(res_rdy, p + 1)
                for t in range(4):
                    dve.bn_stats(st3[:, par, t, :], res[0:T, par, t])
                dve.drain()
                for t in range(4):
                    dve.bn_aggr(mv3[:, par, t, :], st3[:, par, t, :]).then_inc(mv3_rdy, 1)
                if not (at_start(w) and par == 0):
                    shift(p - 1, 1 - par)

            def shift(p, par):
                dve.wait_ge(rstd3_rdy, p + 1)
                dve.scalar_tensor_tensor(nb3[:, par], mv3[:, par, :, 0], -1.0, rstd3[:, par],
                                         ALU.mult, ALU.mult).then_inc(nb3_rdy, 1)
            phase3(dve, out_step)
            shift(NP - 1, 1)

        @block.tensor
        def _(pe):
            pe.wait_ge(loaded, 16 * N_LOADS)
            pe.wait_ge(ident_st, 2)
            for k in range(2):
                mm = pe.matmul(ps[0:G, 0, k * D:(k + 1) * D], wg1[:, k * G:(k + 1) * G], wg2[:, :],
                               start=True, stop=True)
            mm.then_inc(wg_mm, 1)
            pe.wait_ge(sl_st, 5)
            for k in range(2):
                mm = pe.transpose(ps[0:G, 1, k * S:(k + 1) * S], slq[:, k * G:(k + 1) * G], ident[0:S, 0:S])
            mm.then_inc(slT_mm, 1)
            pe.wait_ge(wg_sb, 1)
            pe.wait_ge(slT_sb, 1)
            pe.wait_ge(wo_halved, 1)

            def project(g, weights, done):
                for k in range(2):
                    mm = pe.matmul(ps[0:G, g, 0:PT], weights[0:G, k, g * G:(g + 1) * G], hT[0:G, k],
                                   start=(k == 0), stop=(k == 1))
                mm.then_inc(done, 1)

            def project_out(j):
                pe.wait_ge(og_sb, 2 * j + 2)
                for t in range(4):
                    for k in range(2):
                        mm = pe.matmul(ps[0:T, 2 + t // 2, (t % 2) * D:(t % 2) * D + D],
                                       og[0:G, k, t * T:(t + 1) * T], wo[0:G, k], start=(k == 0), stop=(k == 1))
                    if t % 2:
                        mm.then_inc(wo_mm, 1)

            def embed(i, c, tail):
                pe.wait_ge(x_loaded, 16 * i + 16)
                for g in range(2):
                    if c:
                        pe.wait_ge(qm_sb, 2 * i - 1 + g)
                    if tail:
                        pe.wait_ge((Lc_rdy, DT_sb)[g], i - 1)
                    for k in range(KP):
                        mm = pe.matmul(ps[0:G, g, 0:PT], w_sb[:, k, g * G:(g + 1) * G], x_sb[:, k],
                                       start=(k == 0), stop=(k == KP - 1))
                    mm.then_inc(hT_mm, 1)

            def scores(i, k, c):
                g, a = ORDER[k]
                pe.wait_ge(qm_sb, 2 * i + g + 1)
                for u, (h0, nh, mt, n0, n) in enumerate(UNIT):
                    unit = UNITS * k + u
                    if unit >= SC_BANKS:
                        pe.wait_ge(p_rdy, 4 * UNITS * i + unit - SC_BANKS + 1)
                    elif unit < 2:
                        if c:
                            pe.wait_ge(t1_rdy, 4 * i)
                    else:
                        pe.wait_ge(v_sb, 2 * i + 1)
                    pe.matmul(ps[0:T, 2 + unit % SC_BANKS, 0:nh * n],
                              kT[0:G, g, a * TOK + mt * T:a * TOK + mt * T + T],
                              qm[0:G, g, h0:h0 + nh, a * TOK + n0:a * TOK + n0 + n],
                              start=True, stop=True).then_inc(sc_mm, 1)

            def values(i, k):
                g, a = ORDER[k]
                pe.wait_ge(hb_sb, 2 * i + g + 1)
                pe.wait_ge(v_sb, 2 * i + a + 1)
                pe.wait_ge(p_rdy, 4 * UNITS * i + UNITS * (k + 1))
                for odd in range(2):
                    for mt in range(2):
                        for b in range(HG // 2):
                            h = 2 * b + odd
                            if mt == 0:
                                p = p_sb[0:T, k % 2, b, odd * TOK:(odd + 1) * TOK]
                            else:
                                p = p_sb[0:T, k % 2, 3 + h // 3, (h % 3) * T:(h % 3 + 1) * T]
                            mm = pe.matmul(ps[32 * b:32 * b + 32, 5 + g, a * TOK + mt * T:(a + 1) * TOK],
                                           vpad[0:T, 2 * a + mt, 32 * (g * HG + h):32 * (g * HG + h) + 32], p,
                                           start=(odd == 0 and mt == 0), stop=(odd == 1 and mt == 1))
                mm.then_inc(pv_mm, 1)

            def slot_input_out(j):
                pe.wait_ge(y_sb, j + 1)
                for k in range(2):
                    mm = pe.transpose(ps[0:G, 7, 128 * k:128 * k + 128], ysb[:, k * G:(k + 1) * G], ident[:, :])
                mm.then_inc(yT_mm, 1)
                pe.wait_ge(Cn_rdy, j + 1)
                for k in range(2):
                    mm = pe.transpose(ps[:, 4, k * T:(k + 1) * T], Cn[:, 2 * k:2 * k + 2, :], ident[0:T, 0:T])
                mm.then_inc(cb_mm, 1)

            def token_features(j):
                for t in range(4):
                    pe.wait_ge(tok_rdy, 4 * j + t + 1)
                    for k in range(2):
                        mm = pe.transpose(ps[0:G, k, t * T:(t + 1) * T], tok[0:T, t, k * G:(k + 1) * G],
                                          ident[0:T, 0:T])
                mm.then_inc(tokT_mm, 1)

            def logits(j):
                pe.wait_ge(tokT_sb, j + 1)
                for k in range(2):
                    for a in range(2):
                        mm = pe.matmul(ps[64 * a:64 * a + 64, 7, 0:TOK], slT[:, k, :],
                                       tokT[0:G, k, a * TOK:(a + 1) * TOK], start=(k == 0), stop=(k == 1))
                mm.then_inc(lg_mm, 1)

            def logits_turned(j):
                pe.wait_ge(Ls_rdy, j + 1)
                for k in range(2):
                    mm = pe.transpose(ps[0:T, 0, 128 * k:128 * k + 128], Ls[:, k * T:(k + 1) * T], ident[:, :])
                mm.then_inc(lt_mm, 1)

            def dispatch_turned(j):
                pe.wait_ge(Dn_rdy, j + 1)
                for k in range(2):
                    mm = pe.transpose(ps[0:T, 1, 128 * k:128 * k + 128], Dn[:, k * T:(k + 1) * T], ident[:, :])
                mm.then_inc(dt_mm, 1)

            def slot_inputs(j):
                pe.wait_ge(DT_sb, j + 1)
                for k in range(2):
                    for a in range(2):
                        mm = pe.matmul(ps[64 * a:64 * a + 64, 7, 0:D], DT[:, k, 64 * a:64 * a + 64],
                                       xn[0:T, 2 * a + k], start=(k == 0), stop=(k == 1))
                mm.then_inc(y_mm, 1)

            def step(i, has_a, c, tail):
                j = i - 1
                if has_a:
                    embed(i, c, tail)
                if tail:
                    slot_input_out(i - 2)
                if c:
                    project_out(j)
                if has_a:
                    for g in range(2):
                        pe.wait_ge(hT_sb, 2 * i + 2)
                        project(g, wqkv[:, 1], k_mm)
                    for g in range(2):
                        pe.wait_ge(k_sb, 2 * i + g + 1)
                        project(g, wg, g_mm)
                    for t in range(4):
                        for k in range(2):
                            mm = pe.transpose(ps[0:T, 5 + t // 2, (t % 2) * D + k * G:(t % 2) * D + (k + 1) * G],
                                              hT[0:G, k, t * T:(t + 1) * T], ident[0:G, 0:G])
                        if t % 2:
                            mm.then_inc(ht_mm, 1)
                    for g in range(2):
                        pe.wait_ge(g_sb, 2 * i + g + 1)
                        project(g, wqkv[:, 0], q_mm)
                    for t in range(4):
                        if t == 0 and tail:
                            pe.wait_ge(cb_sb, i - 1)
                        if t == 2 and tail:
                            pe.wait_ge(yT_sb, 2 * i - 2)
                        for k in range(2):
                            mm = pe.matmul(ps[0:T, 4 + 3 * (t // 2), (t % 2) * D:(t % 2) * D + D],
                                           hT[0:G, k, t * T:(t + 1) * T], wqkv[0:G, 2, k],
                                           start=(k == 0), stop=(k == 1))
                        if t % 2:
                            mm.then_inc(v_mm, 1)
                    scores(i, 0, c)
                    pe.wait_ge(qm_sb, 2 * i + 2)
                if c:
                    token_features(j)
                if has_a:
                    scores(i, 1, c)
                if c:
                    if has_a:
                        pe.wait_ge(v_sb, 2 * i + 2)
                    else:
                        pe.wait_ge(yT_sb, 2 * i - 2)
                    logits(j)
                if has_a:
                    values(i, 0)
                    scores(i, 2, c)
                if c:
                    logits_turned(j)
                if has_a:
                    values(i, 1)
                    scores(i, 3, c)
                if c:
                    dispatch_turned(j)
                if has_a:
                    values(i, 2)
                if c:
                    slot_inputs(j)
                if has_a:
                    values(i, 3)
            phase1(pe, step)
            pe.wait_ge(cb_sb, NP)

            def fc2_pair(u, n):
                pe.wait_ge(hgT_rdy, u + 1)
                if not (isinstance(u, int) and u < 2):
                    pe.wait_ge(y2st_rdy, u - 1)
                for k in range(FJ):
                    for s in range(2):
                        mm = pe.matmul(ps[64 * s:64 * s + 64, 4 + n % 2, 0:D], hgT[:, k, 64 * s:64 * s + 64],
                                       w2v[n][:, s, k], start=(k == 0), stop=(k == FJ - 1))
                mm.then_inc(fc2_mm, 1)

            def slot_step(u, n, v):
                start = isinstance(u, int) and u == 0
                pe.wait_ge(w_loaded[n], 48 * v + 48)
                pe.wait_ge(ybuf_rdy, u + 1)
                if not start:
                    pe.wait_ge(gelu_rdy, u)
                for x in range(2):
                    for k in range(2):
                        for s in range(2):
                            mm = pe.matmul(ps[64 * s:64 * s + 64, x, 0:FH], ybuf[0:G + k, n % 2, k, s],
                                           w1v[n][0:G + k, s, k, x * FH:(x + 1) * FH],
                                           start=(k == 0), stop=(k == 1))
                mm.then_inc(fc1_mm, 1)
                if not start:
                    fc2_pair(u - 1, (n - 1) % RING)
                pe.wait_ge(gelu_rdy, u + 1)
                if not start:
                    pe.wait_ge(hgT_rdy, u)
                for k in range(FJ):
                    mm = pe.transpose(ps[:, 2 + k // 3, (k % 3) * 128:(k % 3) * 128 + 128],
                                      hg[:, 128 * k:128 * k + 128], ident[:, :])
                mm.then_inc(tr_mm, 1)
            phase2(pe, slot_step)
            fc2_pair(NU - 1, RING - 1)

            pe.wait_ge(hgT_rdy, NU)
            def out_step(p, par, w):
                pe.wait_ge(cbuf_loaded[par], 16 * w + 16)
                pe.wait_ge(y2b_rdy, p + 1)
                if not at_start(w):
                    pe.wait_ge(res_rdy, p - 1)
                for t in range(4):
                    a, k = t // 2, t % 2
                    mm = pe.matmul(ps[0:T, 2 * par + a, k * D:(k + 1) * D],
                                   cbuf[64 * a:64 * a + 64, par, k * T:(k + 1) * T],
                                   y2b[64 * a:64 * a + 64, par, :], start=True, stop=True)
                mm.then_inc(cmb_mm, 1)
            phase3(pe, out_step)


N_LOADS = 13


def kernel(**inputs):
    import numpy as np
    import concourse.bacc as bacc
    from concourse.bass_utils import run_bass_kernel_spmd

    g = {k: np.asarray(v) for k, v in inputs.items()}
    x = g["x"].reshape(NP, 2, C_IN, GRID, PATCH, GRID, PATCH).transpose(0, 4, 6, 2, 1, 3, 5)
    arrays = {
        "xT": x.reshape(NP, KP, 128, PT).transpose(0, 2, 1, 3),
        "W": g["L0_tok_W"].T.reshape(KP, 128, D).transpose(1, 0, 2),
        "Wqkv": np.stack([g[f"L0_attn_W{n}"].reshape(2, G, D) for n in "qkv"]).transpose(2, 0, 1, 3),
        "Wo": g["L0_attn_Wo"].reshape(2, G, D).transpose(1, 0, 2),
        "Wg1T": g["L0_attn_Wg1"].T,
        "Wg2": g["L0_attn_Wg2"],
        "log_slope": g["L0_attn_log_slope"],
        "ln_w": g["L0_attn_ln_w"],
        "ln_b": g["L0_attn_ln_b"],
        "slots": g["L0_ffn_slots"],
        "scale": g["L0_ffn_scale"].reshape(S, 1),
        "fc1": g["L0_ffn_fc1_weight"].reshape(NU, 2, 2, G, F).transpose(0, 3, 1, 2, 4),
        "fc1b": g["L0_ffn_fc1_bias"].reshape(NU, 1, 2, F),
        "fc2": g["L0_ffn_fc2_weight"].reshape(NU, 2, FJ, 128, D).transpose(0, 3, 1, 2, 4),
        "fc2b": g["L0_ffn_fc2_bias"],
        "norm_w": g["L0_ffn_norm_weight"],
    }
    nc = bacc.Bacc("TRN2", target_bir_lowering=False, num_devices=1)
    feed, aps = {}, []
    for name, a in arrays.items():
        feed[f"in_{name}"] = np.ascontiguousarray(a)
        aps.append(nc.dram_tensor(f"in_{name}", list(a.shape), F32, kind="ExternalInput").ap())
    out = nc.dram_tensor("out", [NB, TOK, D], F32, kind="ExternalOutput").ap()
    vit_tower(nc, *aps, out)
    r = run_bass_kernel_spmd(nc, [feed], core_ids=[0])
    return r.results[0]["out"]
```

```python
from contextlib import ExitStack

import concourse.bass as bass
from concourse import mybir

F32 = mybir.dt.float32
F32R = mybir.dt.float32r
ALU = mybir.AluOpType
ACT = mybir.ActivationFunctionType
AX = mybir.AxisListType.X

NB, C_IN, IMG, PATCH = 64, 3, 224, 16
GRID = IMG // PATCH
TOK = GRID * GRID
T = TOK // 2
PT = 2 * TOK
NP = NB // 2
D = 192
KP = PATCH * PATCH * C_IN // 128
G = D // 2
H = 12
HD = D // H
HG = H // 2
S = 64
F = 768
FH = F // 2
FJ = F // 128
NU = S // 2
RING = 6
TURNS, REST = NU // RING, NU % RING
assert RING % 2 == 0 and REST % 2 == 0
DEEP = 4
REGION = 35640
QM_AT = 4 * (3 * KP * PT + 2 * KP * D + 6 * 2 * D + 9 * 2 * PT)
BANK = 512
EPS = 1e-5
ORDER = [(0, 0), (0, 1), (1, 0), (1, 1)]
UH = HG // 2
UNIT = [(0, 0), (UH, 0), (0, 1), (UH, 1)]
UNITS = len(UNIT)
SC_BANKS = 3


def vit_tower(nc, xT, W, Wqk, Wv, Wo, Wg1T, Wg2, log_slope, row_slope, ln_w, ln_b, slots, scale, fc1, fc2, fc2b,
              norm_w, out):
    h2_dram = nc.dram_tensor("h2_dram", [NP, T, 4, D], F32, kind="Internal").ap()
    comb_dram = nc.dram_tensor("comb_dram", [NP, 128, TOK], F32, kind="Internal").ap()
    y2_dram = nc.dram_tensor("y2_dram", [S, 2, NP, D], F32, kind="Internal").ap()
    y2_rows = y2_dram.rearrange("(u s) a p d -> u (s a p) d", s=2)
    out_v = out.rearrange("b t d -> (b t) d").rearrange("(p x m) d -> p m x d", x=4, m=T)
    with ExitStack() as ctx:
        def sb(name, shape):
            return ctx.enter_context(nc.sbuf_tensor(name, shape, F32))

        def sem(name):
            return ctx.enter_context(nc.semaphore(name))

        ps = ctx.enter_context(nc.psum_tensor("ps", [128, 8, BANK], F32))

        yT = sb("yT", [G + 1, 2, S, NB])
        ident = sb("ident", [128, 128])
        b2 = sb("b2", [128, D])

        region_at = nc.sbuf_base
        assert region_at % 32 == 0, region_at
        fence = sb("fence", [128, REGION])

        def placer(at):
            at = [at]

            def place(name, shape, dtype=F32):
                size = 4
                for n in shape[1:]:
                    size *= n
                t = nc.alloc_sbuf_tensor_at(name, shape, dtype, offset=at[0])
                at[0] += -(-size // 32) * 32
                assert at[0] <= region_at + 4 * fence.shape[1], (name, at[0] - region_at)
                return t
            return place

        place = placer(region_at)
        x_sb = place("x_sb", [128, KP, PT])
        xh, xl = place("xh", [128, KP, PT], F32R), place("xl", [128, KP, PT], F32R)
        wh, wl = place("wh", [128, KP, D], F32R), place("wl", [128, KP, D], F32R)
        pjh, pjl = place("pjh", [G, 3, 2, D], F32R), place("pjl", [G, 3, 2, D], F32R)
        hT = place("hT", [G, 2, PT])
        hTh, hTl = place("hTh", [G, 2, PT], F32R), place("hTl", [G, 2, PT], F32R)
        kT = place("kT", [G, 2, PT])
        kh, kl = place("kh", [G, 2, PT], F32R), place("kl", [G, 2, PT], F32R)
        qT, ql = place("qT", [G, 2, PT]), place("ql", [G, 2, PT])
        qh = place("qh", [G, 2, PT], F32R)
        qmh, qml = place("qmh", [G, 2, HG, PT], F32R), place("qml", [G, 2, HG, PT], F32R)
        qd = place("qd", [G, 2, 2, T])
        vpad = place("vpad", [T, 4, H * 32])
        dec = place("dec", [T, H, T])
        gt = place("gt", [G, 2, PT])
        kts = place("kts", [T, 2, D])
        state = place("state", [G, 4, G])
        wv = place("wv", [G, 2, D])
        p_sb = place("p_sb", [T, 2, UNITS, UH * T])
        place = placer(region_at + QM_AT)
        wst = place("wst", [128, KP, D])
        pst = place("pst", [G, 3, 2, D])
        wg1, wg2 = place("wg1", [16, D]), place("wg2", [16, D])
        sl, slq = place("sl", [S, D]), place("slq", [S, D])
        dist, steps = place("dist", [T, T]), place("steps", [G, T])
        place = placer(region_at)
        w1v, w2v = [], []
        for n in range(RING):
            w1v.append(place(f"w1v{n}", [128, 2, 2, F]))
            w2v.append(place(f"w2v{n}", [128, 2, FJ, D]))
        hg = place("hg", [128, F])
        hgT = place("hgT", [128, FJ, 128])
        y2st = place("y2st", [128, 2, D])
        ybuf = place("ybuf", [G + 1, 2, 2, 2, NB])
        place = placer(region_at)
        y2r = place("y2r", [128, NP, D])
        place = placer(region_at + REST * 4 * (4 * F + 2 * FJ * D))
        cbuf, h2r = place("cbuf", [128, DEEP, TOK]), place("h2r", [T, DEEP, 4, D])
        y2b = place("y2b", [128, DEEP, D])
        res, o_sb = place("res", [T, DEEP, 4, D]), place("o_sb", [T, DEEP, 4, D])

        og = sb("og", [G, 2, PT])
        hb = sb("hb", [T, 4, D])
        t2 = sb("t2", [T, 4, D])
        tok = t2
        h2 = sb("h2", [T, 4, D])
        xn = sb("xn", [T, 4, D])
        tokT = sb("tokT", [G, 2, PT])
        wo = sb("wo", [G, 2, D])
        slT = sb("slT", [G, 2, S])
        mask = sb("mask", [G, HG])
        slope, rslope = sb("slope", [T, H]), sb("rslope", [G, 2])
        left = sb("left", [T, 1])
        kdec = sb("kdec", [T, H])
        qdec = sb("qdec", [G, 2, T])
        lnw, lnb, nw = sb("lnw", [T, D]), sb("lnb", [T, D]), sb("nw", [T, D])
        slst = sb("slst", [S, 4])
        st1, mv1 = sb("st1", [T, 4, 6]), sb("mv1", [T, 4, 2])
        st2, mv2 = sb("st2", [T, 4, 6]), sb("mv2", [T, 4, 2])
        rstd1, rstd2, rr, ms = (sb(n, [T, 4]) for n in ("rstd1", "rstd2", "rr", "ms"))
        ss, nrm, invn = (sb(n, [T, 4]) for n in ("ss", "nrm", "invn"))
        expo = sb("expo", [128, 4, 4])
        ve = sb("ve", [128, 3 + DEEP, 4])
        Ls, Es, Dn = sb("Ls", [128, TOK]), sb("Es", [128, TOK]), sb("Dn", [128, TOK])
        lmx, lneg, lsum, lrec = (sb(n, [128, 1]) for n in ("lmx", "lneg", "lsum", "lrec"))
        DT = sb("DT", [T, 2, 128])
        Lc, Ec, Cn = (sb(n, [T, 4, S]) for n in ("Lc", "Ec", "Cn"))
        cmx, csum, crec = (sb(n, [T, 4]) for n in ("cmx", "csum", "crec"))
        ysb = sb("ysb", [128, D])
        warm = sb("warm", [1, 2])
        cst = sb("cst", [128, TOK])
        st3, mv3 = sb("st3", [T, DEEP, 4, 6]), sb("mv3", [T, DEEP, 4, 2])
        rstd3, nb3 = sb("rstd3", [T, DEEP, 4]), sb("nb3", [T, DEEP, 4])

        loaded, ident_st, mask_st, dist_st = sem("loaded"), sem("ident_st"), sem("mask_st"), sem("dist_st")
        expo_st = sem("expo_st")
        zeroed, dec_exp, dec_rdy = sem("zeroed"), sem("dec_exp"), sem("dec_rdy")
        wg_mm, wg_sb, wo_halved = sem("wg_mm"), sem("wg_sb"), sem("wo_halved")
        sl_st, slT_mm, slT_sb = sem("sl_st"), sem("slT_mm"), sem("slT_sb")
        x_loaded = sem("x_loaded")
        hT_mm, hT_sb = sem("hT_mm"), sem("hT_sb")
        xh_rdy, xl_rdy = sem("xh_rdy"), sem("xl_rdy")
        hTh_rdy, hTl_rdy = sem("hTh_rdy"), sem("hTl_rdy")
        k_mm, k_sb = sem("k_mm"), sem("k_sb")
        kh_rdy, kl_rdy = sem("kh_rdy"), sem("kl_rdy")
        qh_rdy, ql_rdy, qd_rdy = sem("qh_rdy"), sem("ql_rdy"), sem("qd_rdy")
        kt_mm, kts_rdy, s_mm, s_sb = sem("kt_mm"), sem("kts_rdy"), sem("s_mm"), sem("s_sb")
        w_split, tables = sem("w_split"), sem("tables")
        g_mm, g_sb = sem("g_mm"), sem("g_sb")
        q_mm, q_sb = sem("q_mm"), sem("q_sb")
        qmh_rdy, qml_rdy = sem("qmh_rdy"), sem("qml_rdy")
        v_mm, v_sb = sem("v_mm"), sem("v_sb")
        ht_mm, hb_sb = sem("ht_mm"), sem("hb_sb")
        sc_mm, p_rdy = sem("sc_mm"), sem("p_rdy")
        pv_mm, og_sb = sem("pv_mm"), sem("og_sb")
        wo_mm = sem("wo_mm")
        mv1_rdy, rstd1_rdy = sem("mv1_rdy"), sem("rstd1_rdy")
        t1_rdy, t2_rdy = sem("t1_rdy"), sem("t2_rdy")
        mv2_rdy, rstd2_rdy = sem("mv2_rdy"), sem("rstd2_rdy")
        ms_rdy, rr_rdy = sem("ms_rdy"), sem("rr_rdy")
        ve1_rdy, ve2_rdy, ve3_rdy, ve4_rdy = (sem(n) for n in ("ve1_rdy", "ve2_rdy", "ve3_rdy", "ve4_rdy"))
        h2_rdy, xn_rdy, ss_rdy = sem("h2_rdy"), sem("xn_rdy"), sem("ss_rdy")
        nrm_rdy, invn_rdy, tok_rdy = sem("nrm_rdy"), sem("invn_rdy"), sem("tok_rdy")
        h2_stored = sem("h2_stored")
        tokT_mm, tokT_sb = sem("tokT_mm"), sem("tokT_sb")
        lg_mm, Ls_rdy, lmx_rdy, lneg_rdy = (sem(n) for n in ("lg_mm", "Ls_rdy", "lmx_rdy", "lneg_rdy"))
        Es_rdy, lrec_rdy, Dn_rdy = sem("Es_rdy"), sem("lrec_rdy"), sem("Dn_rdy")
        lt_mm, cmx_rdy, Lc_rdy, Ec_rdy = (sem(n) for n in ("lt_mm", "cmx_rdy", "Lc_rdy", "Ec_rdy"))
        csum_rdy, crec_rdy, Cn_rdy = sem("csum_rdy"), sem("crec_rdy"), sem("Cn_rdy")
        dt_mm, DT_sb = sem("dt_mm"), sem("DT_sb")
        y_mm, y_sb, yT_mm, yT_sb = sem("y_mm"), sem("y_sb"), sem("yT_mm"), sem("yT_sb")
        cb_mm, cb_sb, comb_stored = sem("cb_mm"), sem("cb_sb"), sem("comb_stored")
        w_loaded = [sem(f"w_loaded{n}") for n in range(RING)]
        ybuf_rdy, fc1_mm, gelu_rdy = sem("ybuf_rdy"), sem("fc1_mm"), sem("gelu_rdy")
        tr_mm, hgT_rdy, fc2_mm, y2st_rdy = (sem(n) for n in ("tr_mm", "hgT_rdy", "fc2_mm", "y2st_rdy"))
        y2_stored = [sem("y2_stored0"), sem("y2_stored1")]
        h2r_loaded = [sem(f"h2r_loaded{n}") for n in range(DEEP)]
        y2r_loaded = [sem(f"y2r_loaded{n}") for n in range(DEEP)]
        cbuf_loaded = [sem(f"cbuf_loaded{n}") for n in range(DEEP)]
        y2b_rdy, cmb_mm, res_rdy = (sem(n) for n in ("y2b_rdy", "cmb_mm", "res_rdy"))
        mv3_rdy, rstd3_rdy = sem("mv3_rdy"), sem("rstd3_rdy")
        nb3_rdy, o_rdy = sem("nb3_rdy"), sem("o_rdy")
        out_stored = [sem(f"out_stored{n}") for n in range(DEEP)]

        def phase1(eng, step):
            step(0, True, False, False, False, True)
            step(1, True, True, False, False, True)
            step(2, True, True, True, False, True)
            with eng.Fori(3, NP - 1) as i:
                step(i, True, True, True, True, True)
            step(NP - 1, True, True, True, True, False)
            step(NP, False, True, True, True, False)
            step(NP + 1, False, False, True, True, False)

        def phase2(eng, step):
            for n in range(RING):
                step(n, n, 0)
            with eng.Fori(1, TURNS) as v:
                for n in range(RING):
                    step(RING * v + n, n, v)
            for n in range(REST):
                step(RING * TURNS + n, n, TURNS)

        def phase3(eng, step):
            for n in range(DEEP):
                step(n, n, 0)
            with eng.Fori(1, NP // DEEP) as w:
                for n in range(DEEP):
                    step(DEEP * w + n, n, w)

        def at_start(w):
            return isinstance(w, int) and w == 0

        block = ctx.enter_context(nc.Block())

        @block.sync
        def _(sp):
            loads = [
                (wst[:, :, :], W), (pst[:, 0:2], Wqk), (wv[:, :, :], Wv), (wo[:, :, :], Wo), (wg1[:, :], Wg1T),
                (wg2[:, :], Wg2), (slope[:, :], log_slope.partition_broadcast(T)), (rslope[:, :], row_slope),
                (lnw[:, :], ln_w.partition_broadcast(T)), (lnb[:, :], ln_b.partition_broadcast(T)),
                (nw[:, :], norm_w.partition_broadcast(T)), (sl[:, :], slots), (slst[:, 3:4], scale),
                (b2[0:S, :], fc2b), (b2[S:128, :], fc2b),
            ]
            assert len(loads) == N_LOADS
            sp.dma_start(x_sb[:, :, :], xT[0]).then_inc(x_loaded, 16)
            for dst, src in loads:
                sp.dma_start(dst, src).then_inc(loaded, 16)

            def load_weights(u, n):
                sp.dma_start(w1v[n][0:G + 1], fc1[u]).then_inc(w_loaded[n], 16)
                sp.dma_start(w2v[n][:, :, :, :], fc2[u]).then_inc(w_loaded[n], 16)

            def store_h2(j):
                sp.wait_ge(h2_rdy, 4 * j + 4)
                sp.dma_start(h2_dram[j], h2[:, :, :]).then_inc(h2_stored, 16)

            def store_comb(j):
                sp.wait_ge(cb_sb, j + 1)
                sp.dma_start(comb_dram[j], cst[:, :]).then_inc(comb_stored, 16)

            def load_x(i):
                sp.wait_ge(xl_rdy, KP * i)
                sp.dma_start(x_sb[:, :, :], xT[i]).then_inc(x_loaded, 16)

            load_x(1)

            def step(i, c, d):
                if c:
                    store_h2(i - 1)
                load_x(i + 2)
                if d:
                    store_comb(i - 2)

            step(0, False, False)
            step(1, True, False)
            with sp.Fori(2, NP - 2) as i:
                step(i, True, True)
            store_h2(NP - 3)
            store_comb(NP - 4)
            sp.wait_ge(hT_mm, 2 * NP)
            load_weights(0, 0)
            sp.wait_ge(g_mm, 2 * NP)
            load_weights(1, 1)
            store_h2(NP - 2)
            sp.wait_ge(sc_mm, 4 * UNITS * NP)
            load_weights(2, 2)
            store_comb(NP - 3)
            sp.wait_ge(qd_rdy, 2 * NP)
            load_weights(3, 3)
            load_weights(4, 4)
            store_comb(NP - 2)
            sp.wait_ge(pv_mm, 4 * NP)
            sp.wait_ge(og_sb, 2 * NP)
            load_weights(5, 5)
            store_h2(NP - 1)
            store_comb(NP - 1)

            def load_comb(p, n):
                sp.dma_start(cbuf[:, n], comb_dram[p]).then_inc(cbuf_loaded[n], 16)

            def load_h2(p, n):
                sp.dma_start(h2r[:, n], h2_dram[p]).then_inc(h2r_loaded[n], 16)

            def slot_step(u, n, more):
                sp.wait_ge(y2st_rdy, u + 1)
                sp.dma_start(y2_rows[u], y2st[:, n % 2, :]).then_inc(y2_stored[n % 2], 16)
                if more:
                    load_weights(u + RING, n)
            with sp.Fori(0, TURNS - 1) as v:
                for n in range(RING):
                    slot_step(RING * v + n, n, True)
            for n in range(RING):
                slot_step(RING * (TURNS - 1) + n, n, n < REST)

            sp.wait_ge(h2_stored, 16 * NP)
            sp.wait_ge(comb_stored, 16 * NP)
            for n in range(DEEP):
                load_comb(n, n)
                load_h2(n, n)
            for n in range(REST):
                slot_step(RING * TURNS + n, n, False)
            for par in range(2):
                sp.wait_ge(y2_stored[par], 16 * NU // 2)
            for n in range(DEEP):
                c = slice(n * NP // DEEP, (n + 1) * NP // DEEP)
                for a in range(2):
                    sp.dma_start(y2r[64 * a:64 * a + 64, c, :], y2_dram[:, a, c, :]).then_inc(y2r_loaded[n], 16)
            with sp.Fori(0, NP // DEEP - 1) as w:
                for n in range(DEEP):
                    p = DEEP * w + n
                    sp.wait_ge(cmb_mm, p + 1)
                    load_comb(p + DEEP, n)
                    sp.wait_ge(res_rdy, p + 1)
                    load_h2(p + DEEP, n)
            for n in range(DEEP):
                sp.wait_ge(out_stored[n], 16 * (NP // DEEP))

        @block.gpsimd
        def _(pool):
            pool.iota(dist[:, :], [[1, T]], base=0, channel_multiplier=-1,
                      allow_small_or_imprecise_dtypes=True).then_inc(dist_st, 1)
            pool.wait_ge(dist_st, 1)
            pool.iota(steps[:, :], [[1, T]], base=0, channel_multiplier=0,
                      allow_small_or_imprecise_dtypes=True).then_inc(dist_st, 1)
            pool.wait_ge(dist_st, 2)
            pool.iota(left[:, :], [[0, 1]], base=T, channel_multiplier=-1,
                      allow_small_or_imprecise_dtypes=True).then_inc(dist_st, 1)
            pool.wait_ge(ident_st, 1)
            pool.affine_select(out=ident[:, :], in_=ident[:, :], compare_op=ALU.not_equal, fill=1.0, base=0,
                               pattern=[[-1, 128]], channel_multiplier=1).then_inc(ident_st, 1)
            pool.wait_ge(mask_st, 1)
            pool.affine_select(out=mask[:, :], in_=mask[:, :], compare_op=ALU.is_ge, fill=0.0, base=0,
                               pattern=[[-HD, HG]], channel_multiplier=1).then_inc(mask_st, 1)
            pool.wait_ge(mask_st, 2)
            pool.affine_select(out=mask[:, :], in_=mask[:, :], compare_op=ALU.is_ge, fill=0.0, base=HD - 1,
                               pattern=[[HD, HG]], channel_multiplier=-1).then_inc(mask_st, 1)
            pool.wait_ge(dist_st, 3)
            pool.tensor_scalar(dist[:, :], dist[:, :], 0.0, None, ALU.max).then_inc(dist_st, 1)
            pool.wait_ge(sl_st, 1)
            pool.wait_ge(expo_st, 4)
            pool.tensor_tensor(slst[:, 1:2], slst[:, 0:1], expo[0:S, 1, 0:1], ALU.pow).then_inc(sl_st, 1)
            pool.wait_ge(sl_st, 2)
            pool.tensor_scalar(slst[:, 1:2], slst[:, 1:2], EPS, None, ALU.max).then_inc(sl_st, 1)
            pool.wait_ge(dec_exp, H)
            pool.affine_select(out=dec[:, :, :], in_=dec[:, :, :], compare_op=ALU.is_ge, fill=0.0, base=0,
                               pattern=[[0, H], [1, T]], channel_multiplier=-1).then_inc(dec_rdy, 1)

            def split_x(i, chunks):
                for k in chunks:
                    pool.wait_ge(xh_rdy, 2 * i + k // (KP // 2) + 1)
                    pool.tensor_tensor(xl[:, k], x_sb[:, k], xh[:, k].bitcast(F32), ALU.subtract)\
                        .then_inc(xl_rdy, 1)
            split_x(0, range(KP))

            def step(i, a, c, d, d_before, more):
                if c:
                    first_norm(i - 1)
                if d and not a:
                    dispatch_shift(i - 2)
                if a:
                    pool.wait_ge(qh_rdy, i + 1)
                    pool.tensor_tensor(ql[:, :, :], qT[:, :, :], qh[:, :, :].bitcast(F32), ALU.subtract)\
                        .then_inc(ql_rdy, 1)
                    pool.wait_ge(kh_rdy, i + 1)
                    pool.tensor_tensor(kl[:, :, :], kT[:, :, :], kh[:, :, :].bitcast(F32), ALU.subtract)\
                        .then_inc(kl_rdy, 1)
                if c:
                    second_norm(i - 1)
                if a:
                    for g in range(2):
                        pool.wait_ge(q_sb, 2 * i + g + 1)
                        pool.tensor_tensor(qd[:, g], qT[:, g].rearrange("p (a c m) -> p a c m", a=2, c=2)[:, :, 1],
                                           qdec[:, g].unsqueeze(1).to_broadcast([G, 2, T]), ALU.mult)\
                            .then_inc(qd_rdy, 1)
                if more:
                    split_x(i + 1, range(KP // 2))
                if d and a:
                    dispatch_shift(i - 2)
                if d:
                    dispatch_weights(i - 2)
                if more:
                    split_x(i + 1, range(KP // 2, KP))
                if d:
                    combine_weights(i - 2)
                if c:
                    tokens(i - 1)

            def first_norm(j):
                pool.wait_ge(mv1_rdy, 4 * j + 4)
                pool.tensor_tensor(ve[0:T, 0], mv1[:, :, 1], expo[0:T, 3], ALU.add).then_inc(ve1_rdy, 1)
                pool.wait_ge(ve1_rdy, j + 1)
                pool.tensor_tensor(rstd1[:, :], ve[0:T, 0], expo[0:T, 0], ALU.pow).then_inc(rstd1_rdy, 1)

            def second_norm(j):
                pool.wait_ge(mv2_rdy, 4 * j + 4)
                pool.tensor_tensor(ve[0:T, 1], mv2[:, :, 1], expo[0:T, 3], ALU.add).then_inc(ve2_rdy, 1)
                pool.wait_ge(ve2_rdy, j + 1)
                pool.tensor_tensor(rstd2[:, :], ve[0:T, 1], expo[0:T, 0], ALU.pow).then_inc(rstd2_rdy, 1)
                pool.wait_ge(rstd2_rdy, j + 1)
                pool.tensor_tensor(ms[:, :], mv2[:, :, 1], rstd2[:, :], ALU.mult).then_inc(ms_rdy, 1)
                pool.wait_ge(ms_rdy, 2 * j + 1)
                pool.tensor_tensor(ms[:, :], ms[:, :], rstd2[:, :], ALU.mult).then_inc(ms_rdy, 1)
                pool.wait_ge(ms_rdy, 2 * j + 2)
                pool.tensor_tensor(ve[0:T, 2], ms[:, :], expo[0:T, 3], ALU.add).then_inc(ve3_rdy, 1)
                pool.wait_ge(ve3_rdy, j + 1)
                pool.tensor_tensor(rr[:, :], ve[0:T, 2], expo[0:T, 0], ALU.pow).then_inc(rr_rdy, 1)

            def tokens(j):
                pool.wait_ge(nrm_rdy, j + 1)
                pool.tensor_tensor(invn[:, :], nrm[:, :], expo[0:T, 0], ALU.pow).then_inc(invn_rdy, 1)
                pool.wait_ge(invn_rdy, j + 1)
                for t in range(4):
                    pool.tensor_tensor(tok[0:T, t], xn[0:T, t], invn[:, t:t + 1].to_broadcast([T, D]), ALU.mult)\
                        .then_inc(tok_rdy, 1)

            def dispatch_shift(j):
                pool.wait_ge(lmx_rdy, j + 1)
                pool.tensor_tensor(lneg[:, :], lmx[:, :], expo[:, 2, 0:1], ALU.mult).then_inc(lneg_rdy, 1)

            def dispatch_weights(j):
                pool.wait_ge(lrec_rdy, j + 1)
                pool.tensor_tensor(Dn[:, :], Es[:, :], lrec[:, 0:1].to_broadcast([128, TOK]), ALU.mult).then_inc(Dn_rdy, 1)

            def combine_weights(j):
                pool.wait_ge(crec_rdy, j + 1)
                pool.tensor_tensor(Cn[:, :, :], Ec[:, :, :], crec[:, :].unsqueeze(2).to_broadcast([T, 4, S]),
                                   ALU.mult).then_inc(Cn_rdy, 1)
            phase1(pool, step)

            pool.wait_ge(yT_sb, 2 * NP)
            pool.wait_ge(zeroed, 3)

            def slot_step(u, n, v):
                if not (isinstance(u, int) and u < 2):
                    pool.wait_ge(fc1_mm, u - 1)
                src = yT[:, :, :, :].rearrange("p k (u s) b -> p k u s b", s=2)
                pool.tensor_copy(ybuf[:, n % 2], src[:, :, u]).then_inc(ybuf_rdy, 1)
            phase2(pool, slot_step)

            def out_rstd(p, n):
                pool.wait_ge(mv3_rdy, 4 * p + 4)
                pool.tensor_tensor(ve[0:T, 3 + n], mv3[:, n, :, 1], expo[0:T, 3], ALU.add).then_inc(ve4_rdy, 1)
                pool.wait_ge(ve4_rdy, p + 1)
                pool.tensor_tensor(rstd3[:, n], ve[0:T, 3 + n], expo[0:T, 0], ALU.pow).then_inc(rstd3_rdy, 1)

            def bias(p, n):
                pool.tensor_tensor(y2b[:, n], y2r[:, p], b2[:, :], ALU.add).then_inc(y2b_rdy, 1)

            pool.wait_ge(y2r_loaded[0], 32)
            for n in range(DEEP):
                bias(n, n)
            for n in range(1, DEEP):
                pool.wait_ge(y2r_loaded[n], 32)
            with pool.Fori(0, NP // DEEP - 1) as w:
                for n in range(DEEP):
                    p = DEEP * w + n
                    out_rstd(p, n)
                    pool.wait_ge(cmb_mm, p + 1)
                    bias(p + DEEP, n)
            for n in range(DEEP):
                out_rstd(NP - DEEP + n, n)

        @block.scalar
        def _(act):
            act.wait_ge(loaded, 16 * N_LOADS)
            act.wait_ge(dist_st, 4)
            for h in range(H):
                act.activation(dec[:, h, :], dist[:, :], ACT.Exp, scale=slope[:, h:h + 1]).then_inc(dec_exp, 1)
            act.activation(kdec[:, :], slope[:, :], ACT.Exp, scale=left[:, 0:1]).then_inc(tables, 1)
            for g in range(2):
                act.activation(qdec[:, g], steps[:, :], ACT.Exp, scale=rslope[:, g:g + 1]).then_inc(tables, 1)
            act.wait_ge(mask_st, 3)
            act.wait_ge(zeroed, 3)

            def use_table(func):
                act.activation(warm[:, 1:2], warm[:, 0:1], func)

            def round_x(i, k):
                act.wait_ge(x_loaded, 16 * i + 16)
                c = slice(k * KP // 2, (k + 1) * KP // 2)
                act.activation(xh[:, c], x_sb[:, c], ACT.Copy).then_inc(xh_rdy, 1)
            for k in range(2):
                round_x(0, k)

            def step(i, a, c, d, d_before, more):
                if a:
                    act.wait_ge(hT_mm, 2 * i + 1)
                    act.activation(hT[:, 0], ps[0:G, 0, 0:PT], ACT.Copy).then_inc(hT_sb, 1)
                    act.wait_ge(hT_sb, 2 * i + 1)
                    act.activation(hTh[:, 0], hT[:, 0], ACT.Copy).then_inc(hTh_rdy, 1)
                if d:
                    act.wait_ge(tokT_mm, i - 1)
                    act.activation(tokT[:, :, :], ps[0:G, 5:7, 0:PT], ACT.Copy).then_inc(tokT_sb, 1)
                if a:
                    act.wait_ge(hT_mm, 2 * i + 2)
                    act.activation(hT[:, 1], ps[0:G, 1, 0:PT], ACT.Copy).then_inc(hT_sb, 1)
                    act.wait_ge(hT_sb, 2 * i + 2)
                    act.activation(hTh[:, 1], hT[:, 1], ACT.Copy).then_inc(hTh_rdy, 1)
                if more:
                    round_x(i + 1, 0)
                if a:
                    use_table(ACT.Silu)
                if a:
                    for g in range(2):
                        act.wait_ge(q_mm, 2 * i + g + 1)
                        act.activation(qT[:, g], ps[0:G, g, 0:PT], ACT.Silu).then_inc(q_sb, 1)
                    act.wait_ge(q_sb, 2 * i + 2)
                    act.activation(qh[:, :, :], qT[:, :, :], ACT.Copy).then_inc(qh_rdy, 1)
                    for g in range(2):
                        act.wait_ge(k_mm, 2 * i + g + 1)
                        act.activation(kT[:, g], ps[0:G, g, 0:PT], ACT.Silu).then_inc(k_sb, 1)
                    act.wait_ge(k_sb, 2 * i + 2)
                    act.activation(kh[:, :, :], kT[:, :, :], ACT.Copy).then_inc(kh_rdy, 1)
                    masked_queries(i, 0)
                    for g in range(2):
                        act.wait_ge(v_mm, 2 * i + g + 1)
                        dst = vpad[:, 2 * g:2 * g + 2].rearrange("p t (j q d) -> p (t j) q d", q=4, d=HD)
                        src = ps[0:T, 4 + 3 * g, 0:2 * D].rearrange("p (j q d) -> p j q d", q=2, d=HD)
                        act.activation(dst[:, :, 0:4:3, :], src, ACT.Silu).then_inc(v_sb, 1)
                    if c:
                        act.wait_ge(og_sb, 2 * i)
                    for g in range(2):
                        act.wait_ge(g_mm, 2 * i + g + 1)
                        act.activation(gt[:, g], ps[0:G, g, 0:PT], ACT.Tanh, scale=0.5).then_inc(g_sb, 1)
                    masked_queries(i, 1)
                if d:
                    act.wait_ge(lg_mm, i - 1)
                    act.activation(Ls[:, :], ps[:, 7, 0:TOK], ACT.Copy).then_inc(Ls_rdy, 1)
                if more:
                    round_x(i + 1, 1)
                if d:
                    use_table(ACT.Exp)
                    dispatch(i - 2, d_before)

            def dispatch(j, d_before):
                act.wait_ge(lneg_rdy, j + 1)
                act.wait_ge(Ls_rdy, j + 1)
                act.activation(Es[:, :], Ls[:, :], ACT.Exp, bias=lneg[:, 0:1], accum_out=lsum[:, 0:1])\
                    .then_inc(Es_rdy, 1)
                act.wait_ge(Lc_rdy, j + 1)
                act.activation(Ec[:, :, :], Lc[:, :, :], ACT.Exp).then_inc(Ec_rdy, 1)
                act.wait_ge(dt_mm, j + 1)
                act.activation(DT[:, :, :], ps[0:T, 1, 0:256].rearrange("p (c s) -> p c s", c=2),
                               ACT.Copy).then_inc(DT_sb, 1)
                act.wait_ge(y_mm, j + 1)
                act.activation(ysb[:, :], ps[:, 7, 0:D], ACT.Copy).then_inc(y_sb, 1)
                if d_before:
                    act.wait_ge(comb_stored, 16 * j)
                act.wait_ge(cb_mm, j + 1)
                act.activation(cst[:, :], ps[:, 4, 0:TOK], ACT.Copy).then_inc(cb_sb, 1)
                act.wait_ge(yT_mm, j + 1)
                for k in range(2):
                    dst = yT[0:G, k].rearrange("x s (a p) -> x a s p", a=2)[:, :, :, j]
                    src = ps[0:G, 7, 128 * k:128 * k + 128].rearrange("x (a s) -> x a s", a=2)
                    act.activation(dst, src, ACT.Copy).then_inc(yT_sb, 1)

            def masked_queries(i, g):
                for m in range(HG):
                    last = act.activation(qmh[:, g, m], qT[:, g], ACT.Identity, scale=mask[:, m:m + 1])
                last.then_inc(qmh_rdy, 1)
            phase1(act, step)

            def slot_step(u, n, v):
                act.wait_ge(fc1_mm, u + 1)
                act.activation(hg[:, :].rearrange("p (x f) -> p x f", x=2), ps[:, 0:2, 0:FH], ACT.Gelu)\
                    .then_inc(gelu_rdy, 1)
            phase2(act, slot_step)

            def out_step(p, n, w):
                act.wait_ge(nb3_rdy, p + 1)
                act.wait_ge(rstd3_rdy, p + 1)
                if not at_start(w):
                    act.wait_ge(out_stored[n], 16 * w)
                for t in range(4):
                    act.activation(o_sb[:, n, t], res[:, n, t], ACT.Identity,
                                   bias=nb3[:, n, t:t + 1], scale=rstd3[:, n, t:t + 1]).then_inc(o_rdy, 1)
                act.wait_ge(o_rdy, 4 * p + 4)
                act.dma_start(out_v[p], o_sb[:, n]).then_inc(out_stored[n], 16)
            phase3(act, out_step)

        @block.vector
        def _(dve):
            dve.memset(ident[:, :], 0.0).then_inc(ident_st, 1)
            dve.memset(mask[:, :], 1.0).then_inc(mask_st, 1)
            for n, e in enumerate((-0.5, 0.5, -1.0, EPS)):
                dve.memset(expo[:, n], e).then_inc(expo_st, 1)
            dve.memset(warm[:, :], 0.0).then_inc(zeroed, 1)
            dve.memset(vpad[:, :, :], 0.0).then_inc(zeroed, 1)
            dve.memset(yT[G:G + 1, :, :, :], 1.0).then_inc(zeroed, 1)
            dve.wait_ge(loaded, 16 * N_LOADS)
            dve.tensor_scalar(wo[0:G], wo[0:G], 0.5, None, ALU.mult).then_inc(wo_halved, 1)
            dve.tensor_tensor_reduce(out=slq[:, :], in0=sl[:, :], in1=sl[:, :], scale=1.0, scalar=0.0,
                                     op0=ALU.mult, op1=ALU.add, accum_out=slst[:, 0:1]).then_inc(sl_st, 1)
            dve.wait_ge(sl_st, 3)
            dve.reciprocal(slst[:, 2:3], slst[:, 1:2]).then_inc(sl_st, 1)
            dve.wait_ge(sl_st, 4)
            dve.tensor_scalar(slq[:, :], sl[:, :], slst[:, 2:3], slst[:, 3:4], ALU.mult, ALU.mult)\
                .then_inc(sl_st, 1)
            dve.wait_ge(wg_mm, 1)
            dve.tensor_copy(pst[:, 2], ps[0:G, 0, 0:2 * D].rearrange("p (k d) -> p k d", k=2)).then_inc(wg_sb, 1)
            dve.wait_ge(wg_sb, 1)
            dve.tensor_copy(wh[:, :, :], wst[:, :, :]).then_inc(w_split, 1)
            dve.tensor_copy(pjh[:, :, :, :], pst[:, :, :, :]).then_inc(w_split, 1)
            dve.wait_ge(w_split, 2)
            dve.tensor_tensor(wl[:, :, :], wst[:, :, :], wh[:, :, :].bitcast(F32), ALU.subtract).then_inc(w_split, 1)
            dve.tensor_tensor(pjl[:, :, :, :], pst[:, :, :, :], pjh[:, :, :, :].bitcast(F32), ALU.subtract)\
                .then_inc(w_split, 1)
            dve.wait_ge(slT_mm, 1)
            dve.tensor_copy(slT[:, :, :], ps[0:G, 1, 0:2 * S].rearrange("p (k s) -> p k s", k=2))\
                .then_inc(slT_sb, 1)
            dve.wait_ge(dec_rdy, 1)
            dve.wait_ge(tables, 3)

            def statistics(j, x):
                dve.wait_ge(wo_mm, 2 * j + x + 1)
                for t in (2 * x, 2 * x + 1):
                    dve.bn_stats(st1[:, t, :], ps[0:T, 2 + x, (t % 2) * D:(t % 2) * D + D])

            def first_norm(j, d):
                dve.drain()
                for t in range(4):
                    dve.bn_aggr(mv1[:, t, :], st1[:, t, :]).then_inc(mv1_rdy, 1)
                if d:
                    dve.wait_ge(tokT_mm, j)
                for t in range(4):
                    dve.wait_ge(mv1_rdy, 4 * j + t + 1)
                    dve.scalar_tensor_tensor(t2[0:T, t], ps[0:T, 2 + t // 2, (t % 2) * D:(t % 2) * D + D],
                                             mv1[:, t, 0:1], lnw[:, :], ALU.subtract, ALU.mult)\
                        .then_inc(t1_rdy, 1)

            def residual(j):
                dve.wait_ge(rstd1_rdy, j + 1)
                for t in range(4):
                    dve.wait_ge(t1_rdy, 4 * j + t + 1)
                    dve.scalar_tensor_tensor(t2[0:T, t], t2[0:T, t], rstd1[:, t:t + 1], hb[0:T, t],
                                             ALU.mult, ALU.add).then_inc(t2_rdy, 1)
                for t in range(4):
                    dve.wait_ge(t2_rdy, 4 * j + t + 1)
                    dve.bn_stats(st2[:, t, :], t2[0:T, t])
                dve.drain()
                for t in range(4):
                    dve.bn_aggr(mv2[:, t, :], st2[:, t, :]).then_inc(mv2_rdy, 1)

            def second_norm(j):
                dve.wait_ge(mv2_rdy, 4 * j + 4)
                dve.wait_ge(rstd2_rdy, j + 1)
                if not (isinstance(j, int) and j == 0):
                    dve.wait_ge(h2_stored, 16 * j)
                for t in range(4):
                    dve.tensor_scalar(h2[0:T, t], t2[0:T, t], mv2[:, t, 0:1], rstd2[:, t:t + 1],
                                      ALU.subtract, ALU.mult).then_inc(h2_rdy, 1)

            def slot_tokens(j, d):
                dve.wait_ge(rr_rdy, j + 1)
                if d:
                    dve.wait_ge(y_mm, j)
                for t in range(4):
                    dve.wait_ge(h2_rdy, 4 * j + t + 1)
                    dve.scalar_tensor_tensor(xn[0:T, t], h2[0:T, t], rr[:, t:t + 1], nw[:, :],
                                             ALU.mult, ALU.mult).then_inc(xn_rdy, 1)
                for t in range(4):
                    dve.wait_ge(xn_rdy, 4 * j + t + 1)
                    dve.tensor_tensor_reduce(out=tok[0:T, t], in0=xn[0:T, t], in1=xn[0:T, t], scale=1.0,
                                             scalar=0.0, op0=ALU.mult, op1=ALU.add,
                                             accum_out=ss[:, t:t + 1]).then_inc(ss_rdy, 1)
                dve.wait_ge(ss_rdy, 4 * j + 4)
                dve.tensor_scalar(nrm[:, :], ss[:, :], EPS * EPS, None, ALU.max).then_inc(nrm_rdy, 1)

            def decay(i, k, units=range(UNITS)):
                g, a = ORDER[k]
                if k >= 2:
                    dve.wait_ge(pv_mm, 4 * i + k - 1)
                for u in units:
                    h0 = UNIT[u][0]
                    dve.wait_ge(sc_mm, 4 * UNITS * i + UNITS * k + u + 1)
                    src = ps[0:T, 2 + (UNITS * k + u) % SC_BANKS, 0:UH * T].rearrange("p (h n) -> p h n", h=UH)
                    dst = p_sb[:, k % 2, u].rearrange("p (h n) -> p h n", h=UH)
                    dve.tensor_tensor(dst, src, dec[:, g * HG + h0:g * HG + h0 + UH], ALU.mult).then_inc(p_rdy, 1)

            def masked_queries(g, heads):
                for m in heads:
                    last = dve.tensor_scalar(qml[:, g, m], ql[:, g], mask[:, m:m + 1], None, ALU.mult)
                if HG - 1 in heads:
                    last.then_inc(qml_rdy, 1)

            def gated(i, g):
                dve.wait_ge(pv_mm, 4 * i + 2 * g + 2)
                dve.wait_ge(g_sb, 2 * i + g + 1)
                dve.scalar_tensor_tensor(og[:, g], gt[:, g], 1.0, ps[0:G, 5 + g, 0:PT],
                                         ALU.add, ALU.mult).then_inc(og_sb, 1)

            def maxima(j):
                dve.wait_ge(Ls_rdy, j + 1)
                dve.reduce_max(lmx[:, :], Ls[:, :], AX).then_inc(lmx_rdy, 1)
                dve.wait_ge(lt_mm, j + 1)
                lt = ps[0:T, 0, 0:256].rearrange("p (x s) -> p x s", s=S)
                dve.reduce_max(cmx[:, :], lt, AX).then_inc(cmx_rdy, 1)
                dve.wait_ge(cmx_rdy, j + 1)
                dve.tensor_tensor(Lc[:, :, :], lt, cmx[:, :].unsqueeze(2).to_broadcast([T, 4, S]),
                                  ALU.subtract).then_inc(Lc_rdy, 1)

            def sums(j):
                dve.wait_ge(Es_rdy, j + 1)
                dve.reciprocal(lrec[:, :], lsum[:, :]).then_inc(lrec_rdy, 1)
                dve.wait_ge(Ec_rdy, j + 1)
                dve.reduce_sum(csum[:, :], Ec[:, :, :], AX).then_inc(csum_rdy, 1)
                dve.wait_ge(csum_rdy, j + 1)
                dve.reciprocal(crec[:, :], csum[:, :]).then_inc(crec_rdy, 1)

            def step(i, a, c, d, d_before, more):
                if d and not (a or c):
                    maxima(i - 2)
                    sums(i - 2)
                for g in range(2):
                    if c and g == 0:
                        statistics(i - 1, 0)
                    if a:
                        dve.wait_ge(hTh_rdy, 2 * i + g + 1)
                        dve.tensor_tensor(hTl[:, g], hT[:, g], hTh[:, g].bitcast(F32), ALU.subtract)\
                            .then_inc(hTl_rdy, 1)
                if c:
                    statistics(i - 1, 1)
                    first_norm(i - 1, d)
                    if not a:
                        maxima(i - 2)
                    residual(i - 1)
                    if not a:
                        sums(i - 2)
                if a:
                    for x in range(2):
                        dve.wait_ge(ht_mm, 2 * i + x + 1)
                        dve.tensor_tensor(hb[:, 2 * x:2 * x + 2],
                                          ps[0:T, 5 + x, 0:2 * D].rearrange("p (t d) -> p t d", t=2),
                                          lnb[:, :].unsqueeze(1).to_broadcast([T, 2, D]), ALU.add)\
                            .then_inc(hb_sb, 1)
                    dve.wait_ge(ql_rdy, i + 1)
                    masked_queries(0, range(HG))
                    masked_queries(1, range(UH))
                    dve.wait_ge(kt_mm, i + 1)
                    dve.tensor_tensor(kts[:, :, :].rearrange("p a (h d) -> p a h d", h=H),
                                      ps[0:T, 5, 0:2 * D].rearrange("p (a h d) -> p a h d", a=2, h=H),
                                      kdec[:, :].unsqueeze(1).unsqueeze(3).to_broadcast([T, 2, H, HD]),
                                      ALU.mult).then_inc(kts_rdy, 1)
                    decay(i, 0)
                    masked_queries(1, range(UH, HG))
                    decay(i, 1, range(2))
                    dve.wait_ge(s_mm, i + 1)
                    dve.tensor_tensor(state[:, :, :].rearrange("p x (h d) -> p x h d", h=HG),
                                      ps[0:G, 6, 0:4 * G].rearrange("p (x h d) -> p x h d", x=4, h=HG),
                                      mask[:, :].unsqueeze(1).unsqueeze(3).to_broadcast([G, 4, HG, HD]),
                                      ALU.mult).then_inc(s_sb, 1)
                    decay(i, 1, range(2, UNITS))
                if d and a:
                    maxima(i - 2)
                if a:
                    decay(i, 2)
                if d and a:
                    sums(i - 2)
                if c:
                    second_norm(i - 1)
                if a:
                    decay(i, 3)
                    gated(i, 0)
                if c:
                    slot_tokens(i - 1, d)
                if a:
                    gated(i, 1)
            phase1(dve, step)

            def slot_step(u, n, v):
                par = n % 2
                dve.wait_ge(tr_mm, u + 1)
                dve.tensor_copy(hgT[:, :, :].rearrange("p (x j) b -> p x (j b)", x=2), ps[:, 2:4, 0:FH])\
                    .then_inc(hgT_rdy, 1)
                if not (isinstance(u, int) and u < 2):
                    dve.wait_ge(y2_stored[par], 16 * (RING // 2 * v + n // 2))
                dve.wait_ge(fc2_mm, u + 1)
                dve.tensor_copy(y2st[:, par], ps[:, 4 + par, 0:D]).then_inc(y2st_rdy, 1)
            phase2(dve, slot_step)

            def out_step(p, n, w):
                dve.wait_ge(cmb_mm, p + 1)
                dve.wait_ge(h2r_loaded[n], 16 * w + 16)
                if not at_start(w):
                    dve.wait_ge(o_rdy, 4 * (p + 1 - DEEP))
                dve.tensor_tensor(res[0:T, n].rearrange("p (x t) d -> p x (t d)", x=2),
                                  ps[0:T, 2 * n:2 * n + 2, 0:2 * D],
                                  h2r[:, n].rearrange("p (x t) d -> p x (t d)", x=2), ALU.add)\
                    .then_inc(res_rdy, 1)
                dve.wait_ge(res_rdy, p + 1)
                for t in range(4):
                    dve.bn_stats(st3[:, n, t, :], res[0:T, n, t])
                dve.drain()
                for t in range(4):
                    dve.bn_aggr(mv3[:, n, t, :], st3[:, n, t, :]).then_inc(mv3_rdy, 1)
                if not (at_start(w) and n == 0):
                    shift(p - 1, (n - 1) % DEEP)

            def shift(p, n):
                dve.wait_ge(rstd3_rdy, p + 1)
                dve.scalar_tensor_tensor(nb3[:, n], mv3[:, n, :, 0], -1.0, rstd3[:, n],
                                         ALU.mult, ALU.mult).then_inc(nb3_rdy, 1)
            phase3(dve, out_step)
            shift(NP - 1, DEEP - 1)

        @block.tensor
        def _(pe):
            pe.wait_ge(loaded, 16 * N_LOADS)
            pe.wait_ge(ident_st, 2)
            for k in range(2):
                mm = pe.matmul(ps[0:G, 0, k * D:(k + 1) * D], wg1[:, k * G:(k + 1) * G], wg2[:, :],
                               start=True, stop=True)
            mm.then_inc(wg_mm, 1)
            pe.wait_ge(sl_st, 5)
            for k in range(2):
                mm = pe.transpose(ps[0:G, 1, k * S:(k + 1) * S], slq[:, k * G:(k + 1) * G], ident[0:S, 0:S])
            mm.then_inc(slT_mm, 1)
            pe.wait_ge(wg_sb, 1)
            pe.wait_ge(w_split, 4)
            pe.wait_ge(slT_sb, 1)
            pe.wait_ge(wo_halved, 1)

            def product(out, hi, lo, x_hi, x_lo, start, stop):
                pe.matmul(out, hi, x_lo, start=start, stop=False)
                pe.matmul(out, lo, x_hi, start=False, stop=False)
                return pe.matmul(out, hi, x_hi, start=False, stop=stop)

            def project(i, g, n, done):
                for k in range(2):
                    pe.wait_ge(hTl_rdy, 2 * i + k + 1)
                    c = slice(g * G, (g + 1) * G)
                    mm = product(ps[0:G, g, 0:PT], pjh[:, n, k, c], pjl[:, n, k, c], hTh[:, k], hTl[:, k],
                                 k == 0, k == 1)
                mm.then_inc(done, 1)

            def project_out(j, x):
                pe.wait_ge(og_sb, 2 * j + 2)
                for t in (2 * x, 2 * x + 1):
                    for k in range(2):
                        mm = pe.matmul(ps[0:T, 2 + x, (t % 2) * D:(t % 2) * D + D],
                                       og[0:G, k, t * T:(t + 1) * T], wo[0:G, k], start=(k == 0), stop=(k == 1))
                mm.then_inc(wo_mm, 1)

            def embed(i, g, c):
                if c:
                    pe.wait_ge(g_sb, 2 * i - 1 + g)
                for k in range(KP):
                    if g == 0:
                        pe.wait_ge(xl_rdy, KP * i + k + 1)
                    c = slice(g * G, (g + 1) * G)
                    mm = product(ps[0:G, g, 0:PT], wh[:, k, c], wl[:, k, c], xh[:, k], xl[:, k],
                                 k == 0, k == KP - 1)
                mm.then_inc(hT_mm, 1)

            def scores(i, k, c):
                g, a = ORDER[k]
                pe.wait_ge(kl_rdy, i + 1)
                pe.wait_ge(qmh_rdy, 2 * i + g + 1)
                pe.wait_ge(qml_rdy, 2 * i + g + 1)
                for u, (h0, mt) in enumerate(UNIT):
                    unit = UNITS * k + u
                    if unit >= SC_BANKS:
                        pe.wait_ge(p_rdy, 4 * UNITS * i + unit - SC_BANKS + 1)
                    elif unit < 2:
                        if c:
                            pe.wait_ge(t1_rdy, 4 * i)
                    else:
                        pe.wait_ge(v_sb, 2 * i + 1)
                    n = slice(a * TOK + mt * T, a * TOK + mt * T + T)
                    h = slice(h0, h0 + UH)
                    product(ps[0:T, 2 + unit % SC_BANKS, 0:UH * T].rearrange("p (h n) -> p h n", h=UH),
                            kh[:, g, n], kl[:, g, n], qmh[:, g, h, n], qml[:, g, h, n],
                            True, True).then_inc(sc_mm, 1)

            def keys_turned(i):
                pe.wait_ge(hb_sb, 2 * i + 2)
                for a in range(2):
                    for g in range(2):
                        mm = pe.transpose(ps[0:T, 5, a * D + g * G:a * D + (g + 1) * G],
                                          kT[:, g, a * TOK:a * TOK + T], ident[0:G, 0:G])
                mm.then_inc(kt_mm, 1)

            def states(i):
                pe.wait_ge(kts_rdy, i + 1)
                pe.wait_ge(v_sb, 2 * i + 2)
                for g, a in ORDER:
                    v = vpad[:, 2 * a].rearrange("p (j q d) -> p j q d", q=4, d=HD)
                    mm = pe.matmul(ps[0:G, 6, (2 * g + a) * G:(2 * g + a + 1) * G]
                                   .rearrange("p (j q d) -> p j q d", q=2, d=HD),
                                   kts[:, a, g * G:(g + 1) * G], v[:, 3 * g:3 * g + 3, 0:4:3, :],
                                   start=True, stop=True)
                mm.then_inc(s_mm, 1)

            def values(i, k):
                g, a = ORDER[k]
                pe.wait_ge(s_sb, i + 1)
                pe.wait_ge(qd_rdy, 2 * i + g + 1)
                pe.wait_ge(p_rdy, 4 * UNITS * i + UNITS * (k + 1))
                for mt in range(2):
                    out = [ps[32 * b:32 * b + 32, 5 + g, a * TOK + mt * T:a * TOK + mt * T + T]
                           for b in range(HG // 2)]
                    for odd in range(2):
                        for b in range(HG // 2):
                            h = 2 * b + odd
                            mm = pe.matmul(out[b], vpad[:, 2 * a + mt, 32 * (g * HG + h):32 * (g * HG + h) + 32],
                                           p_sb[:, k % 2, 2 * mt + h // UH, (h % UH) * T:(h % UH + 1) * T],
                                           start=(odd == 0), stop=(odd == 1 and mt == 0))
                    if mt == 1:
                        for b in range(HG // 2):
                            mm = pe.matmul(out[b], state[:, 2 * g + a, 32 * b:32 * b + 32], qd[:, g, a],
                                           start=False, stop=True)
                mm.then_inc(pv_mm, 1)

            def slot_inputs_turned(j):
                pe.wait_ge(y_sb, j + 1)
                for k in range(2):
                    mm = pe.transpose(ps[0:G, 7, 128 * k:128 * k + 128], ysb[:, k * G:(k + 1) * G], ident[:, :])
                mm.then_inc(yT_mm, 1)

            def combine_turned(j):
                pe.wait_ge(Cn_rdy, j + 1)
                for k in range(2):
                    mm = pe.transpose(ps[:, 4, k * T:(k + 1) * T], Cn[:, 2 * k:2 * k + 2, :], ident[0:T, 0:T])
                mm.then_inc(cb_mm, 1)

            def token_features(j):
                for t in range(4):
                    pe.wait_ge(tok_rdy, 4 * j + t + 1)
                    for k in range(2):
                        mm = pe.transpose(ps[0:G, 5 + k, t * T:(t + 1) * T], tok[0:T, t, k * G:(k + 1) * G],
                                          ident[0:T, 0:T])
                mm.then_inc(tokT_mm, 1)

            def logits(j):
                pe.wait_ge(tokT_sb, j + 1)
                for k in range(2):
                    for a in range(2):
                        mm = pe.matmul(ps[64 * a:64 * a + 64, 7, 0:TOK], slT[:, k, :],
                                       tokT[0:G, k, a * TOK:(a + 1) * TOK], start=(k == 0), stop=(k == 1))
                mm.then_inc(lg_mm, 1)

            def logits_turned(j):
                pe.wait_ge(Ls_rdy, j + 1)
                for k in range(2):
                    mm = pe.transpose(ps[0:T, 0, 128 * k:128 * k + 128], Ls[:, k * T:(k + 1) * T], ident[:, :])
                mm.then_inc(lt_mm, 1)

            def dispatch_turned(j):
                pe.wait_ge(Dn_rdy, j + 1)
                for k in range(2):
                    mm = pe.transpose(ps[0:T, 1, 128 * k:128 * k + 128], Dn[:, k * T:(k + 1) * T], ident[:, :])
                mm.then_inc(dt_mm, 1)

            def slot_inputs(j):
                pe.wait_ge(DT_sb, j + 1)
                for k in range(2):
                    for a in range(2):
                        mm = pe.matmul(ps[64 * a:64 * a + 64, 7, 0:D], DT[:, k, 64 * a:64 * a + 64],
                                       xn[0:T, 2 * a + k], start=(k == 0), stop=(k == 1))
                mm.then_inc(y_mm, 1)

            def step(i, a, c, d, d_before, more):
                if a:
                    embed(i, 0, c)
                if c:
                    project_out(i - 1, 0)
                    if not a:
                        project_out(i - 1, 1)
                if d:
                    if c:
                        pe.wait_ge(og_sb, 2 * i)
                    token_features(i - 2)
                if a:
                    embed(i, 1, c)
                if a and c:
                    project_out(i - 1, 1)
                if a:
                    pe.wait_ge(hT_sb, 2 * i + 2)
                    if d:
                        pe.wait_ge(tokT_sb, i - 1)
                    for t in range(4):
                        for k in range(2):
                            mm = pe.transpose(ps[0:T, 5 + t // 2, (t % 2) * D + k * G:(t % 2) * D + (k + 1) * G],
                                              hT[:, k, t * T:(t + 1) * T], ident[0:G, 0:G])
                        if t % 2:
                            mm.then_inc(ht_mm, 1)
                    for g in range(2):
                        project(i, g, 0, q_mm)
                    for g in range(2):
                        pe.wait_ge(q_sb, 2 * i + g + 1)
                        project(i, g, 1, k_mm)
                    for t in range(4):
                        if t == 0 and d_before:
                            pe.wait_ge(cb_sb, i - 2)
                        if t == 2 and d_before:
                            pe.wait_ge(yT_sb, 2 * i - 4)
                        for k in range(2):
                            mm = pe.matmul(ps[0:T, 4 + 3 * (t // 2), (t % 2) * D:(t % 2) * D + D],
                                           hT[:, k, t * T:(t + 1) * T], wv[:, k], start=(k == 0), stop=(k == 1))
                        if t % 2:
                            mm.then_inc(v_mm, 1)
                    for g in range(2):
                        pe.wait_ge(k_sb, 2 * i + g + 1)
                        project(i, g, 2, g_mm)
                    keys_turned(i)
                    scores(i, 0, c)
                    states(i)
                if d:
                    if a:
                        pe.wait_ge(v_sb, 2 * i + 2)
                    else:
                        pe.wait_ge(yT_sb, 2 * i - 4)
                    logits(i - 2)
                if a:
                    scores(i, 1, c)
                    pe.wait_ge(g_sb, 2 * i + 2)
                if d:
                    logits_turned(i - 2)
                if a:
                    values(i, 0)
                    scores(i, 2, c)
                    values(i, 1)
                if d:
                    dispatch_turned(i - 2)
                if a:
                    scores(i, 3, c)
                    values(i, 2)
                if d:
                    slot_inputs(i - 2)
                if a:
                    values(i, 3)
                if d:
                    if not a:
                        pe.wait_ge(cb_sb, i - 2)
                    combine_turned(i - 2)
                    slot_inputs_turned(i - 2)
            phase1(pe, step)
            pe.wait_ge(cb_sb, NP)

            def fc2_pair(u, n):
                pe.wait_ge(hgT_rdy, u + 1)
                if not (isinstance(u, int) and u < 2):
                    pe.wait_ge(y2st_rdy, u - 1)
                for k in range(FJ):
                    for s in range(2):
                        mm = pe.matmul(ps[64 * s:64 * s + 64, 4 + n % 2, 0:D], hgT[:, k, 64 * s:64 * s + 64],
                                       w2v[n][:, s, k], start=(k == 0), stop=(k == FJ - 1))
                mm.then_inc(fc2_mm, 1)

            def slot_step(u, n, v):
                start = isinstance(u, int) and u == 0
                pe.wait_ge(w_loaded[n], 32 * v + 32)
                pe.wait_ge(ybuf_rdy, u + 1)
                if not start:
                    pe.wait_ge(gelu_rdy, u)
                for x in range(2):
                    for k in range(2):
                        for s in range(2):
                            mm = pe.matmul(ps[64 * s:64 * s + 64, x, 0:FH], ybuf[0:G + k, n % 2, k, s],
                                           w1v[n][0:G + k, s, k, x * FH:(x + 1) * FH],
                                           start=(k == 0), stop=(k == 1))
                mm.then_inc(fc1_mm, 1)
                if not start:
                    fc2_pair(u - 1, (n - 1) % RING)
                pe.wait_ge(gelu_rdy, u + 1)
                if not start:
                    pe.wait_ge(hgT_rdy, u)
                for k in range(FJ):
                    mm = pe.transpose(ps[:, 2 + k // 3, (k % 3) * 128:(k % 3) * 128 + 128],
                                      hg[:, 128 * k:128 * k + 128], ident[:, :])
                mm.then_inc(tr_mm, 1)
            phase2(pe, slot_step)
            fc2_pair(NU - 1, (NU - 1) % RING)

            pe.wait_ge(hgT_rdy, NU)
            def out_step(p, n, w):
                pe.wait_ge(cbuf_loaded[n], 16 * w + 16)
                pe.wait_ge(y2b_rdy, p + 1)
                if not at_start(w):
                    pe.wait_ge(res_rdy, p + 1 - DEEP)
                for t in range(4):
                    a, k = t // 2, t % 2
                    mm = pe.matmul(ps[0:T, 2 * n + a, k * D:(k + 1) * D],
                                   cbuf[64 * a:64 * a + 64, n, k * T:(k + 1) * T],
                                   y2b[64 * a:64 * a + 64, n, :], start=True, stop=True)
                mm.then_inc(cmb_mm, 1)
            phase3(pe, out_step)


N_LOADS = 15


def kernel(**inputs):
    import numpy as np
    import concourse.bacc as bacc
    from concourse.bass_utils import run_bass_kernel_spmd

    g = {k: np.asarray(v) for k, v in inputs.items()}
    x = g["x"].reshape(NP, 2, C_IN, GRID, PATCH, GRID, PATCH).transpose(0, 4, 6, 2, 1, 3, 5)
    arrays = {
        "xT": x.reshape(NP, KP, 128, PT).transpose(0, 2, 1, 3),
        "W": g["L0_tok_W"].T.reshape(KP, 128, D).transpose(1, 0, 2),
        "Wqk": np.stack([g[f"L0_attn_W{n}"].reshape(2, G, D) for n in "qk"]).transpose(2, 0, 1, 3),
        "Wv": g["L0_attn_Wv"].reshape(2, G, D).transpose(1, 0, 2),
        "Wo": g["L0_attn_Wo"].reshape(2, G, D).transpose(1, 0, 2),
        "Wg1T": g["L0_attn_Wg1"].T,
        "Wg2": g["L0_attn_Wg2"],
        "log_slope": g["L0_attn_log_slope"],
        "row_slope": np.repeat(g["L0_attn_log_slope"], HD).reshape(2, G).T,
        "ln_w": g["L0_attn_ln_w"],
        "ln_b": g["L0_attn_ln_b"],
        "slots": g["L0_ffn_slots"],
        "scale": g["L0_ffn_scale"].reshape(S, 1),
        "fc1": np.concatenate([
            g["L0_ffn_fc1_weight"].reshape(NU, 2, 2, G, F).transpose(0, 3, 1, 2, 4),
            np.stack([np.zeros((NU, 1, 2, F), np.float32), g["L0_ffn_fc1_bias"].reshape(NU, 1, 2, F)], axis=3),
        ], axis=1),
        "fc2": g["L0_ffn_fc2_weight"].reshape(NU, 2, FJ, 128, D).transpose(0, 3, 1, 2, 4),
        "fc2b": g["L0_ffn_fc2_bias"],
        "norm_w": g["L0_ffn_norm_weight"],
    }
    nc = bacc.Bacc("TRN2", target_bir_lowering=False, num_devices=1)
    feed, aps = {}, []
    for name, a in arrays.items():
        feed[f"in_{name}"] = np.ascontiguousarray(a)
        aps.append(nc.dram_tensor(f"in_{name}", list(a.shape), F32, kind="ExternalInput").ap())
    out = nc.dram_tensor("out", [NB, TOK, D], F32, kind="ExternalOutput").ap()
    vit_tower(nc, *aps, out)
    r = run_bass_kernel_spmd(nc, [feed], core_ids=[0])
    return r.results[0]["out"]
```

```python
from contextlib import ExitStack

import concourse.bass as bass
from concourse import mybir

F32 = mybir.dt.float32
F32R = mybir.dt.float32r
ALU = mybir.AluOpType
ACT = mybir.ActivationFunctionType
AX = mybir.AxisListType.X

NB, C_IN, IMG, PATCH = 64, 3, 224, 16
GRID = IMG // PATCH
TOK = GRID * GRID
T = TOK // 2
PT = 2 * TOK
NP = NB // 2
D = 192
KP = PATCH * PATCH * C_IN // 128
G = D // 2
H = 12
HD = D // H
HG = H // 2
RANK = 16
ZL, ZT = 32, 64
ZK = ZT + RANK
S = 64
F = 768
FH = F // 2
FJ = F // 128
NU = S // 2
RING = 6
TURNS, REST = NU // RING, NU % RING
assert RING % 2 == 0 and REST % 2 == 0
DEEP = 4
REGION = 36240
QM_AT = 4 * (3 * KP * PT + 2 * KP * D + 2 * 2 * (2 * D + RANK) + 9 * 2 * PT)
BANK = 512
EPS = 1e-5
ORDER = [(0, 0), (0, 1), (1, 0), (1, 1)]
UH = HG // 2
LOW = 2
EARLY = (3, 2)
UNIT = [(0, 0), (UH, 0), (0, 1), (UH, 1)]
UNITS = len(UNIT)
SC_BANKS = 3


def vit_tower(nc, xT, W, Wq, Wk, Wv, Wo, Wg1, Wg2, log_slope, row_slope, ln_w, ln_b, slots, scale, fc1, fc2, fc2b,
              norm_w, out):
    h2_dram = nc.dram_tensor("h2_dram", [NP, T, 4, D], F32, kind="Internal").ap()
    comb_dram = nc.dram_tensor("comb_dram", [NP, 128, TOK], F32, kind="Internal").ap()
    y2_dram = nc.dram_tensor("y2_dram", [S, 2, NP, D], F32, kind="Internal").ap()
    y2_rows = y2_dram.rearrange("(u s) a p d -> u (s a p) d", s=2)
    out_v = out.rearrange("b t d -> (b t) d").rearrange("(p x m) d -> p m x d", x=4, m=T)
    with ExitStack() as ctx:
        def sb(name, shape):
            return ctx.enter_context(nc.sbuf_tensor(name, shape, F32))

        def sem(name):
            return ctx.enter_context(nc.semaphore(name))

        ps = ctx.enter_context(nc.psum_tensor("ps", [128, 8, BANK], F32))

        yT = sb("yT", [G, 2, S, NB])
        ident = sb("ident", [128, 128])
        b2 = sb("b2", [128, D])

        region_at = nc.sbuf_base
        assert region_at % 32 == 0, region_at
        fence = sb("fence", [128, REGION])

        def placer(at):
            at = [at]

            def place(name, shape, dtype=F32):
                size = 4
                for n in shape[1:]:
                    size *= n
                t = nc.alloc_sbuf_tensor_at(name, shape, dtype, offset=at[0])
                at[0] += -(-size // 32) * 32
                assert at[0] <= region_at + 4 * fence.shape[1], (name, at[0] - region_at)
                return t
            return place

        place = placer(region_at)
        x_sb = place("x_sb", [128, KP, PT])
        xh, xl = place("xh", [128, KP, PT], F32R), place("xl", [128, KP, PT], F32R)
        wh, wl = place("wh", [128, KP, D], F32R), place("wl", [128, KP, D], F32R)
        wqh, wql = place("wqh", [G, 2, D + RANK], F32R), place("wql", [G, 2, D + RANK], F32R)
        wkh, wkl = place("wkh", [G, 2, D], F32R), place("wkl", [G, 2, D], F32R)
        hT = place("hT", [G, 2, PT])
        hTh, hTl = place("hTh", [G, 2, PT], F32R), place("hTl", [G, 2, PT], F32R)
        kT = place("kT", [G, 2, PT])
        kh, kl = place("kh", [G, 2, PT], F32R), place("kl", [G, 2, PT], F32R)
        qT, ql = place("qT", [G, 2, PT]), place("ql", [G, 2, PT])
        qh = place("qh", [G, 2, PT], F32R)
        qmh, qml = place("qmh", [G, 2, HG, PT], F32R), place("qml", [G, 2, HG, PT], F32R)
        qd = place("qd", [G, 2, 2, T])
        vpad = place("vpad", [T, 4, H * 32])
        dec = place("dec", [T, H, T])
        gt = place("gt", [G, 2, PT])
        zt, zs, gw = place("zt", [RANK, PT]), place("zs", [ZK, PT], F32R), place("gw", [ZK, D], F32R)
        kts = place("kts", [T, 2, D])
        state = place("state", [G, 4, G])
        wv = place("wv", [G, 2, D])
        p_sb = place("p_sb", [T, 2, UNITS, UH * T])
        place = placer(region_at + QM_AT)
        wst = place("wst", [128, KP, D])
        wqst, wkst, gst = place("wqst", [G, 2, D + RANK]), place("wkst", [G, 2, D]), place("gst", [ZK, D])
        sl, slq = place("sl", [S, D]), place("slq", [S, D])
        dist, steps = place("dist", [T, T]), place("steps", [G, T])
        place = placer(region_at)
        w1v, w2v = [], []
        for n in range(RING):
            w1v.append(place(f"w1v{n}", [128, 2, 2, F]))
            w2v.append(place(f"w2v{n}", [128, 2, FJ, D]))
        hg = place("hg", [128, F])
        hgT = place("hgT", [128, FJ, 128])
        y2st = place("y2st", [128, 2, D])
        ybuf = place("ybuf", [G + 1, 2, 2, 2, NB])
        place = placer(region_at)
        y2r = place("y2r", [128, NP, D])
        place = placer(region_at + REST * 4 * (4 * F + 2 * FJ * D))
        cbuf, h2r = place("cbuf", [128, DEEP, TOK]), place("h2r", [T, DEEP, 4, D])
        y2b = place("y2b", [128, DEEP, D])
        res, o_sb = place("res", [T, DEEP, 4, D]), place("o_sb", [T, DEEP, 4, D])

        og = sb("og", [G, 2, PT])
        hb = sb("hb", [T, 4, D])
        t2 = sb("t2", [T, 4, D])
        tok = t2
        h2 = sb("h2", [T, 4, D])
        xn = sb("xn", [T, 4, D])
        tokT = sb("tokT", [G, 2, PT])
        wo = sb("wo", [G, 2, D])
        slT = sb("slT", [G, 2, S])
        mask = sb("mask", [G, HG])
        slope, rslope = sb("slope", [T, H]), sb("rslope", [G, 2])
        left = sb("left", [T, 1])
        kdec = sb("kdec", [T, H])
        qdec = sb("qdec", [G, 2, T])
        lnw, lnb, nw = sb("lnw", [T, D]), sb("lnb", [T, D]), sb("nw", [T, D])
        slst = sb("slst", [S, 4])
        st1, mv1 = sb("st1", [T, 4, 6]), sb("mv1", [T, 4, 2])
        st2, mv2 = sb("st2", [T, 4, 6]), sb("mv2", [T, 4, 2])
        rstd1, rstd2, rr, ms = (sb(n, [T, 4]) for n in ("rstd1", "rstd2", "rr", "ms"))
        ss, nrm, invn = (sb(n, [T, 4]) for n in ("ss", "nrm", "invn"))
        expo = sb("expo", [128, 4, 4])
        ve = sb("ve", [128, 3 + DEEP, 4])
        Ls, Es, Dn = sb("Ls", [128, TOK]), sb("Es", [128, TOK]), sb("Dn", [128, TOK])
        lmx, lneg, lsum, lrec = (sb(n, [128, 1]) for n in ("lmx", "lneg", "lsum", "lrec"))
        DT = sb("DT", [T, 2, 128])
        Lc, Ec, Cn = (sb(n, [T, 4, S]) for n in ("Lc", "Ec", "Cn"))
        cmx, csum, crec = (sb(n, [T, 4]) for n in ("cmx", "csum", "crec"))
        ysb = sb("ysb", [128, D])
        warm = sb("warm", [1, 2])
        cst = sb("cst", [128, TOK])
        st3, mv3 = sb("st3", [T, DEEP, 4, 6]), sb("mv3", [T, DEEP, 4, 2])
        rstd3, nb3 = sb("rstd3", [T, DEEP, 4]), sb("nb3", [T, DEEP, 4])

        first_loaded, gst_zeroed = sem("first_loaded"), sem("gst_zeroed")
        loaded, ident_st, mask_st, dist_st = sem("loaded"), sem("ident_st"), sem("mask_st"), sem("dist_st")
        expo_st = sem("expo_st")
        zeroed, dec_exp, dec_rdy = sem("zeroed"), sem("dec_exp"), sem("dec_rdy")
        wo_halved, ones_rdy = sem("wo_halved"), sem("ones_rdy")
        sl_st, slT_mm, slT_sb = sem("sl_st"), sem("slT_mm"), sem("slT_sb")
        x_loaded = sem("x_loaded")
        hT_mm, hT_sb = sem("hT_mm"), sem("hT_sb")
        xh_rdy, xl_rdy = sem("xh_rdy"), sem("xl_rdy")
        hTh_rdy, hTl_rdy = sem("hTh_rdy"), sem("hTl_rdy")
        k_mm, k_sb = sem("k_mm"), sem("k_sb")
        kh_rdy, kl_rdy = sem("kh_rdy"), sem("kl_rdy")
        qh_rdy, ql_rdy, qd_rdy = sem("qh_rdy"), sem("ql_rdy"), sem("qd_rdy")
        kt_mm, kts_rdy, s_mm, s_sb = sem("kt_mm"), sem("kts_rdy"), sem("s_mm"), sem("s_sb")
        w_split, tables = sem("w_split"), sem("tables")
        z_sb, zh_rdy, zl_rdy = sem("z_sb"), sem("zh_rdy"), sem("zl_rdy")
        g_mm, g_sb = sem("g_mm"), sem("g_sb")
        q_mm, q_sb = sem("q_mm"), sem("q_sb")
        qmh_rdy, dqmh_rdy = sem("qmh_rdy"), sem("dqmh_rdy")
        qml_rdy, qml1_rdy = sem("qml_rdy"), sem("qml1_rdy")
        v_mm, v_sb = sem("v_mm"), sem("v_sb")
        ht_mm, hb_sb = sem("ht_mm"), sem("hb_sb")
        sc_mm, p_rdy = sem("sc_mm"), sem("p_rdy")
        pv_mm, og_sb = sem("pv_mm"), sem("og_sb")
        wo_mm = sem("wo_mm")
        mv1_rdy, rstd1_rdy = sem("mv1_rdy"), sem("rstd1_rdy")
        t1_rdy, t2_rdy = sem("t1_rdy"), sem("t2_rdy")
        mv2_rdy, rstd2_rdy = sem("mv2_rdy"), sem("rstd2_rdy")
        ms_rdy, rr_rdy = sem("ms_rdy"), sem("rr_rdy")
        ve1_rdy, ve2_rdy, ve3_rdy, ve4_rdy = (sem(n) for n in ("ve1_rdy", "ve2_rdy", "ve3_rdy", "ve4_rdy"))
        h2_rdy, xn_rdy, ss_rdy = sem("h2_rdy"), sem("xn_rdy"), sem("ss_rdy")
        nrm_rdy, invn_rdy, tok_rdy = sem("nrm_rdy"), sem("invn_rdy"), sem("tok_rdy")
        h2_stored = sem("h2_stored")
        tokT_mm, tokT_sb = sem("tokT_mm"), sem("tokT_sb")
        lg_mm, Ls_rdy, lmx_rdy, lneg_rdy = (sem(n) for n in ("lg_mm", "Ls_rdy", "lmx_rdy", "lneg_rdy"))
        Es_rdy, lrec_rdy, Dn_rdy = sem("Es_rdy"), sem("lrec_rdy"), sem("Dn_rdy")
        lt_mm, cmx_rdy, Lc_rdy, Ec_rdy = (sem(n) for n in ("lt_mm", "cmx_rdy", "Lc_rdy", "Ec_rdy"))
        csum_rdy, crec_rdy, Cn_rdy = sem("csum_rdy"), sem("crec_rdy"), sem("Cn_rdy")
        dt_mm, DT_sb = sem("dt_mm"), sem("DT_sb")
        y_mm, y_sb, yT_mm, yT_sb = sem("y_mm"), sem("y_sb"), sem("yT_mm"), sem("yT_sb")
        cb_mm, cb_sb, comb_stored = sem("cb_mm"), sem("cb_sb"), sem("comb_stored")
        w_loaded = [sem(f"w_loaded{n}") for n in range(RING)]
        ybuf_rdy, fc1_mm, gelu_rdy = sem("ybuf_rdy"), sem("fc1_mm"), sem("gelu_rdy")
        tr_mm, hgT_rdy, fc2_mm, y2st_rdy = (sem(n) for n in ("tr_mm", "hgT_rdy", "fc2_mm", "y2st_rdy"))
        y2_stored = [sem("y2_stored0"), sem("y2_stored1")]
        h2r_loaded = [sem(f"h2r_loaded{n}") for n in range(DEEP)]
        y2r_loaded = [sem(f"y2r_loaded{n}") for n in range(DEEP)]
        cbuf_loaded = [sem(f"cbuf_loaded{n}") for n in range(DEEP)]
        y2b_rdy, cmb_mm, res_rdy = (sem(n) for n in ("y2b_rdy", "cmb_mm", "res_rdy"))
        mv3_rdy, rstd3_rdy = sem("mv3_rdy"), sem("rstd3_rdy")
        nb3_rdy, o_rdy = sem("nb3_rdy"), sem("o_rdy")
        out_stored = [sem(f"out_stored{n}") for n in range(DEEP)]

        def phase1(eng, step):
            step(0, True, False, False, False, True)
            step(1, True, True, False, False, True)
            step(2, True, True, True, False, True)
            with eng.Fori(3, NP - 1) as i:
                step(i, True, True, True, True, True)
            step(NP - 1, True, True, True, True, False)
            step(NP, False, True, True, True, False)
            step(NP + 1, False, False, True, True, False)

        def phase2(eng, step):
            for n in range(RING):
                step(n, n, 0)
            with eng.Fori(1, TURNS) as v:
                for n in range(RING):
                    step(RING * v + n, n, v)
            for n in range(REST):
                step(RING * TURNS + n, n, TURNS)

        def phase3(eng, step):
            for n in range(DEEP):
                step(n, n, 0)
            with eng.Fori(1, NP // DEEP) as w:
                for n in range(DEEP):
                    step(DEEP * w + n, n, w)

        def at_start(w):
            return isinstance(w, int) and w == 0

        block = ctx.enter_context(nc.Block())

        @block.sync
        def _(sp):
            first = [(slope[:, :], log_slope.partition_broadcast(T)), (rslope[:, :], row_slope), (wst[:, :, :], W)]
            assert len(first) == N_FIRST
            loads = [
                (wqst[:, :, 0:D], Wq), (wqst[:, :, D:D + RANK], Wg1), (wkst[:, :, :], Wk), (wv[:, :, :], Wv),
                (lnb[:, :], ln_b.partition_broadcast(T)), (wo[:, :, :], Wo), (lnw[:, :], ln_w.partition_broadcast(T)),
                (nw[:, :], norm_w.partition_broadcast(T)), (sl[:, :], slots), (slst[:, 3:4], scale),
                (b2[0:S, :], fc2b), (b2[S:128, :], fc2b),
            ] + [(gst[r:r + RANK, :], Wg2) for r in (0, ZL, ZT)]
            assert len(loads) == N_LOADS
            for dst, src in first:
                sp.dma_start(dst, src).then_inc(first_loaded, 16)
            sp.dma_start(x_sb[:, :, :], xT[0]).then_inc(x_loaded, 16)
            sp.wait_ge(gst_zeroed, 1)
            for dst, src in loads:
                sp.dma_start(dst, src).then_inc(loaded, 16)

            def load_weights(u, n):
                sp.dma_start(w1v[n][0:G + 1], fc1[u]).then_inc(w_loaded[n], 16)
                sp.dma_start(w2v[n][:, :, :, :], fc2[u]).then_inc(w_loaded[n], 16)

            def store_h2(j):
                sp.wait_ge(h2_rdy, 4 * j + 4)
                sp.dma_start(h2_dram[j], h2[:, :, :]).then_inc(h2_stored, 16)

            def store_comb(j):
                sp.wait_ge(cb_sb, j + 1)
                sp.dma_start(comb_dram[j], cst[:, :]).then_inc(comb_stored, 16)

            def load_x(i):
                sp.wait_ge(xl_rdy, KP * i)
                sp.dma_start(x_sb[:, :, :], xT[i]).then_inc(x_loaded, 16)

            load_x(1)

            def step(i, c, d):
                if c:
                    store_h2(i - 1)
                load_x(i + 2)
                if d:
                    store_comb(i - 2)

            step(0, False, False)
            step(1, True, False)
            with sp.Fori(2, NP - 2) as i:
                step(i, True, True)
            store_h2(NP - 3)
            store_comb(NP - 4)
            sp.wait_ge(hT_mm, 2 * NP)
            load_weights(0, 0)
            sp.wait_ge(g_mm, 2 * NP)
            load_weights(1, 1)
            store_h2(NP - 2)
            sp.wait_ge(sc_mm, 4 * UNITS * NP)
            load_weights(2, 2)
            store_comb(NP - 3)
            sp.wait_ge(qd_rdy, 2 * NP)
            load_weights(3, 3)
            load_weights(4, 4)
            store_comb(NP - 2)
            sp.wait_ge(pv_mm, 4 * NP)
            sp.wait_ge(og_sb, 2 * NP)
            load_weights(5, 5)
            store_h2(NP - 1)
            store_comb(NP - 1)

            def load_comb(p, n):
                sp.dma_start(cbuf[:, n], comb_dram[p]).then_inc(cbuf_loaded[n], 16)

            def load_h2(p, n):
                sp.dma_start(h2r[:, n], h2_dram[p]).then_inc(h2r_loaded[n], 16)

            def slot_step(u, n, more):
                sp.wait_ge(y2st_rdy, u + 1)
                sp.dma_start(y2_rows[u], y2st[:, n % 2, :]).then_inc(y2_stored[n % 2], 16)
                if more:
                    load_weights(u + RING, n)
            with sp.Fori(0, TURNS - 1) as v:
                for n in range(RING):
                    slot_step(RING * v + n, n, True)
            for n in range(RING):
                slot_step(RING * (TURNS - 1) + n, n, n < REST)

            sp.wait_ge(h2_stored, 16 * NP)
            sp.wait_ge(comb_stored, 16 * NP)
            for n in range(DEEP):
                load_comb(n, n)
                load_h2(n, n)
            for n in range(REST):
                slot_step(RING * TURNS + n, n, False)
            for par in range(2):
                sp.wait_ge(y2_stored[par], 16 * NU // 2)
            for n in range(DEEP):
                c = slice(n * NP // DEEP, (n + 1) * NP // DEEP)
                for a in range(2):
                    sp.dma_start(y2r[64 * a:64 * a + 64, c, :], y2_dram[:, a, c, :]).then_inc(y2r_loaded[n], 16)
            with sp.Fori(0, NP // DEEP - 1) as w:
                for n in range(DEEP):
                    p = DEEP * w + n
                    sp.wait_ge(cmb_mm, p + 1)
                    load_comb(p + DEEP, n)
                    sp.wait_ge(res_rdy, p + 1)
                    load_h2(p + DEEP, n)
            for n in range(DEEP):
                sp.wait_ge(out_stored[n], 16 * (NP // DEEP))

        @block.gpsimd
        def _(pool):
            pool.iota(dist[:, :], [[1, T]], base=0, channel_multiplier=-1,
                      allow_small_or_imprecise_dtypes=True).then_inc(dist_st, 1)
            pool.wait_ge(dist_st, 1)
            pool.iota(steps[:, :], [[1, T]], base=0, channel_multiplier=0,
                      allow_small_or_imprecise_dtypes=True).then_inc(dist_st, 1)
            pool.wait_ge(dist_st, 2)
            pool.iota(left[:, :], [[0, 1]], base=T, channel_multiplier=-1,
                      allow_small_or_imprecise_dtypes=True).then_inc(dist_st, 1)
            pool.wait_ge(ident_st, 1)
            pool.affine_select(out=ident[:, :], in_=ident[:, :], compare_op=ALU.not_equal, fill=1.0, base=0,
                               pattern=[[-1, 128]], channel_multiplier=1).then_inc(ident_st, 1)
            pool.wait_ge(mask_st, 1)
            pool.affine_select(out=mask[:, :], in_=mask[:, :], compare_op=ALU.is_ge, fill=0.0, base=0,
                               pattern=[[-HD, HG]], channel_multiplier=1).then_inc(mask_st, 1)
            pool.wait_ge(mask_st, 2)
            pool.affine_select(out=mask[:, :], in_=mask[:, :], compare_op=ALU.is_ge, fill=0.0, base=HD - 1,
                               pattern=[[HD, HG]], channel_multiplier=-1).then_inc(mask_st, 1)
            pool.wait_ge(dist_st, 3)
            pool.tensor_scalar(dist[:, :], dist[:, :], 0.0, None, ALU.max).then_inc(dist_st, 1)
            def split_x(i, chunks):
                for k in chunks:
                    pool.wait_ge(xh_rdy, 2 * i + k // (KP // 2) + 1)
                    pool.tensor_tensor(xl[:, k], x_sb[:, k], xh[:, k].bitcast(F32), ALU.subtract)\
                        .then_inc(xl_rdy, 1)
            split_x(0, range(KP))
            pool.wait_ge(dec_exp, H)
            pool.affine_select(out=dec[:, :, :], in_=dec[:, :, :], compare_op=ALU.is_ge, fill=0.0, base=0,
                               pattern=[[0, H], [1, T]], channel_multiplier=-1).then_inc(dec_rdy, 1)
            pool.wait_ge(sl_st, 1)
            pool.wait_ge(expo_st, 4)
            pool.tensor_tensor(slst[:, 1:2], slst[:, 0:1], expo[0:S, 1, 0:1], ALU.pow).then_inc(sl_st, 1)
            pool.wait_ge(sl_st, 2)
            pool.tensor_scalar(slst[:, 1:2], slst[:, 1:2], EPS, None, ALU.max).then_inc(sl_st, 1)

            def step(i, a, c, d, d_before, more):
                if c:
                    first_norm(i - 1)
                if d and not a:
                    dispatch_shift(i - 2)
                    dispatch_weights(i - 2)
                    combine_weights(i - 2)
                if a:
                    for g in range(2):
                        pool.wait_ge(qh_rdy, 2 * i + g + 1)
                        pool.tensor_tensor(ql[:, g], qT[:, g], qh[:, g].bitcast(F32), ALU.subtract)\
                            .then_inc(ql_rdy, 1)
                    low_keys(i, 0)
                    pool.wait_ge(ql_rdy, 2 * i + 2)
                    for m in range(LOW, HG):
                        pool.tensor_tensor(qml[:, 1, m], ql[:, 1], mask[:, m:m + 1].to_broadcast([G, PT]), ALU.mult)\
                            .then_inc(qml1_rdy, 1)
                    low_keys(i, 1)
                    pool.wait_ge(kl_rdy, 2 * i + 2)
                    pool.wait_ge(zh_rdy, 2 * i + 1)
                    pool.tensor_tensor(zs[ZL:ZL + RANK, :], zt[:, :], zs[0:RANK, :].bitcast(F32), ALU.subtract)\
                        .then_inc(zl_rdy, 1)
                    pool.wait_ge(zl_rdy, i + 1)
                    for g in range(2):
                        pool.wait_ge(q_sb, 2 * i + g + 1)
                        pool.tensor_tensor(qd[:, g], qT[:, g].rearrange("p (a c m) -> p a c m", a=2, c=2)[:, :, 1],
                                           qdec[:, g].unsqueeze(1).to_broadcast([G, 2, T]), ALU.mult)\
                            .then_inc(qd_rdy, 1)
                if c:
                    second_norm(i - 1)
                if d and a:
                    dispatch_shift(i - 2)
                if c:
                    square_norm(i - 1)
                if d and a:
                    dispatch_weights(i - 2)
                if more:
                    split_x(i + 1, range(KP // 2))
                if d and a:
                    combine_weights(i - 2)
                if more:
                    split_x(i + 1, range(KP // 2, KP))
                if c:
                    tokens(i - 1)

            def low_keys(i, g):
                pool.wait_ge(kh_rdy, 2 * i + g + 1)
                pool.tensor_tensor(kl[:, g], kT[:, g], kh[:, g].bitcast(F32), ALU.subtract).then_inc(kl_rdy, 1)

            def first_norm(j):
                for x in range(2):
                    c = slice(2 * x, 2 * x + 2)
                    pool.wait_ge(mv1_rdy, 4 * j + 2 * x + 2)
                    pool.tensor_tensor(ve[0:T, 0, c], mv1[:, c, 1], expo[0:T, 3, c], ALU.add).then_inc(ve1_rdy, 1)
                    pool.wait_ge(ve1_rdy, 2 * j + x + 1)
                    pool.tensor_tensor(rstd1[:, c], ve[0:T, 0, c], expo[0:T, 0, c], ALU.pow).then_inc(rstd1_rdy, 1)

            def second_norm(j):
                pool.wait_ge(mv2_rdy, 4 * j + 4)
                pool.tensor_tensor(ve[0:T, 1], mv2[:, :, 1], expo[0:T, 3], ALU.add).then_inc(ve2_rdy, 1)
                pool.wait_ge(ve2_rdy, j + 1)
                pool.tensor_tensor(rstd2[:, :], ve[0:T, 1], expo[0:T, 0], ALU.pow).then_inc(rstd2_rdy, 1)

            def square_norm(j):
                pool.wait_ge(rstd2_rdy, j + 1)
                pool.tensor_tensor(ms[:, :], mv2[:, :, 1], rstd2[:, :], ALU.mult).then_inc(ms_rdy, 1)
                pool.wait_ge(ms_rdy, 2 * j + 1)
                pool.tensor_tensor(ms[:, :], ms[:, :], rstd2[:, :], ALU.mult).then_inc(ms_rdy, 1)
                pool.wait_ge(ms_rdy, 2 * j + 2)
                pool.tensor_tensor(ve[0:T, 2], ms[:, :], expo[0:T, 3], ALU.add).then_inc(ve3_rdy, 1)
                pool.wait_ge(ve3_rdy, j + 1)
                pool.tensor_tensor(rr[:, :], ve[0:T, 2], expo[0:T, 0], ALU.pow).then_inc(rr_rdy, 1)

            def tokens(j):
                pool.wait_ge(nrm_rdy, j + 1)
                pool.tensor_tensor(invn[:, :], nrm[:, :], expo[0:T, 0], ALU.pow).then_inc(invn_rdy, 1)
                pool.wait_ge(invn_rdy, j + 1)
                for t in range(4):
                    pool.tensor_tensor(tok[0:T, t], xn[0:T, t], invn[:, t:t + 1].to_broadcast([T, D]), ALU.mult)\
                        .then_inc(tok_rdy, 1)

            def dispatch_shift(j):
                pool.wait_ge(lmx_rdy, j + 1)
                pool.tensor_tensor(lneg[:, :], lmx[:, :], expo[:, 2, 0:1], ALU.mult).then_inc(lneg_rdy, 1)

            def dispatch_weights(j):
                pool.wait_ge(lrec_rdy, j + 1)
                pool.tensor_tensor(Dn[:, :], Es[:, :], lrec[:, 0:1].to_broadcast([128, TOK]), ALU.mult).then_inc(Dn_rdy, 1)

            def combine_weights(j):
                pool.wait_ge(crec_rdy, j + 1)
                pool.tensor_tensor(Cn[:, :, :], Ec[:, :, :], crec[:, :].unsqueeze(2).to_broadcast([T, 4, S]),
                                   ALU.mult).then_inc(Cn_rdy, 1)
            phase1(pool, step)

            pool.wait_ge(yT_sb, 2 * NP)

            def slot_step(u, n, v):
                if not (isinstance(u, int) and u < 2):
                    pool.wait_ge(fc1_mm, u - 1)
                src = yT[:, :, :, :].rearrange("p k (u s) b -> p k u s b", s=2)
                pool.tensor_copy(ybuf[0:G, n % 2], src[:, :, u]).then_inc(ybuf_rdy, 1)
            phase2(pool, slot_step)

            def out_rstd(p, n):
                pool.wait_ge(mv3_rdy, 4 * p + 4)
                pool.tensor_tensor(ve[0:T, 3 + n], mv3[:, n, :, 1], expo[0:T, 3], ALU.add).then_inc(ve4_rdy, 1)
                pool.wait_ge(ve4_rdy, p + 1)
                pool.tensor_tensor(rstd3[:, n], ve[0:T, 3 + n], expo[0:T, 0], ALU.pow).then_inc(rstd3_rdy, 1)

            def bias(p, n):
                pool.tensor_tensor(y2b[:, n], y2r[:, p], b2[:, :], ALU.add).then_inc(y2b_rdy, 1)

            pool.wait_ge(y2r_loaded[0], 32)
            for n in range(DEEP):
                bias(n, n)
            for n in range(1, DEEP):
                pool.wait_ge(y2r_loaded[n], 32)
            with pool.Fori(0, NP // DEEP - 1) as w:
                for n in range(DEEP):
                    p = DEEP * w + n
                    out_rstd(p, n)
                    pool.wait_ge(cmb_mm, p + 1)
                    bias(p + DEEP, n)
            for n in range(DEEP):
                out_rstd(NP - DEEP + n, n)

        @block.scalar
        def _(act):
            act.wait_ge(first_loaded, 16 * N_FIRST)
            act.wait_ge(dist_st, 4)
            for h in range(H):
                act.activation(dec[:, h, :], dist[:, :], ACT.Exp, scale=slope[:, h:h + 1]).then_inc(dec_exp, 1)
            act.activation(kdec[:, :], slope[:, :], ACT.Exp, scale=left[:, 0:1]).then_inc(tables, 1)
            for g in range(2):
                act.activation(qdec[:, g], steps[:, :], ACT.Exp, scale=rslope[:, g:g + 1]).then_inc(tables, 1)
            act.wait_ge(mask_st, 3)
            act.wait_ge(zeroed, 2)

            def use_table(func):
                act.activation(warm[:, 1:2], warm[:, 0:1], func)

            def round_x(i, k):
                act.wait_ge(x_loaded, 16 * i + 16)
                c = slice(k * KP // 2, (k + 1) * KP // 2)
                act.activation(xh[:, c], x_sb[:, c], ACT.Copy).then_inc(xh_rdy, 1)
            for k in range(2):
                round_x(0, k)

            def step(i, a, c, d, d_before, more):
                if a:
                    act.wait_ge(hT_mm, 2 * i + 1)
                    act.activation(hT[:, 0], ps[0:G, 0, 0:PT], ACT.Copy).then_inc(hT_sb, 1)
                    act.wait_ge(hT_sb, 2 * i + 1)
                    act.activation(hTh[:, 0], hT[:, 0], ACT.Copy).then_inc(hTh_rdy, 1)
                if d:
                    act.wait_ge(tokT_mm, i - 1)
                    act.activation(tokT[:, :, :], ps[0:G, 5:7, 0:PT], ACT.Copy).then_inc(tokT_sb, 1)
                if a:
                    act.wait_ge(hT_mm, 2 * i + 2)
                    act.activation(hT[:, 1], ps[0:G, 1, 0:PT], ACT.Copy).then_inc(hT_sb, 1)
                    act.wait_ge(hT_sb, 2 * i + 2)
                    act.activation(hTh[:, 1], hT[:, 1], ACT.Copy).then_inc(hTh_rdy, 1)
                    use_table(ACT.Silu)
                if a:
                    for g in range(2):
                        act.wait_ge(q_mm, 2 * i + g + 1)
                        act.activation(qT[:, g], ps[0:G, g, 0:PT], ACT.Silu).then_inc(q_sb, 1)
                    act.wait_ge(q_sb, 2 * i + 2)
                    for g in range(2):
                        act.activation(qh[:, g], qT[:, g], ACT.Copy).then_inc(qh_rdy, 1)
                    for g in range(2):
                        act.wait_ge(k_mm, 2 * i + g + 1)
                        act.activation(kT[:, g], ps[0:G, g, 0:PT], ACT.Silu).then_inc(k_sb, 1)
                    act.wait_ge(k_sb, 2 * i + 2)
                    act.activation(kh[:, 0], kT[:, 0], ACT.Copy).then_inc(kh_rdy, 1)
                    masked_queries(0, range(EARLY[0], HG))
                    for g in range(2):
                        act.wait_ge(v_mm, 2 * i + g + 1)
                        dst = vpad[:, 2 * g:2 * g + 2].rearrange("p t (j q d) -> p (t j) q d", q=4, d=HD)
                        src = ps[0:T, 4 + 3 * g, 0:2 * D].rearrange("p (j q d) -> p j q d", q=2, d=HD)
                        act.activation(dst[:, :, 0:4:3, :], src, ACT.Silu).then_inc(v_sb, 1)
                    act.activation(kh[:, 1], kT[:, 1], ACT.Copy).then_inc(kh_rdy, 1)
                    act.wait_ge(z_sb, i + 1)
                    for row in (0, ZT):
                        act.activation(zs[row:row + RANK, :], zt[:, :], ACT.Copy).then_inc(zh_rdy, 1)
                    masked_queries(1, range(EARLY[1], HG))
                if d:
                    act.wait_ge(lg_mm, i - 1)
                    act.activation(Ls[:, :], ps[:, 7, 0:TOK], ACT.Copy).then_inc(Ls_rdy, 1)
                if more:
                    round_x(i + 1, 0)
                if a:
                    if c:
                        act.wait_ge(og_sb, 2 * i)
                    for g in range(2):
                        act.wait_ge(g_mm, 2 * i + g + 1)
                        act.activation(gt[:, g], ps[0:G, g, 0:PT], ACT.Tanh, scale=0.5).then_inc(g_sb, 1)
                if d:
                    use_table(ACT.Exp)
                    exponentials(i - 2)
                if more:
                    round_x(i + 1, 1)
                if d:
                    dispatch(i - 2, d_before)

            def exponentials(j):
                act.wait_ge(lneg_rdy, j + 1)
                act.wait_ge(Ls_rdy, j + 1)
                act.activation(Es[:, :], Ls[:, :], ACT.Exp, bias=lneg[:, 0:1], accum_out=lsum[:, 0:1])\
                    .then_inc(Es_rdy, 1)
                act.wait_ge(Lc_rdy, j + 1)
                act.activation(Ec[:, :, :], Lc[:, :, :], ACT.Exp).then_inc(Ec_rdy, 1)

            def dispatch(j, d_before):
                act.wait_ge(dt_mm, j + 1)
                act.activation(DT[:, :, :], ps[0:T, 1, 0:256].rearrange("p (c s) -> p c s", c=2),
                               ACT.Copy).then_inc(DT_sb, 1)
                act.wait_ge(y_mm, j + 1)
                act.activation(ysb[:, :], ps[:, 7, 0:D], ACT.Copy).then_inc(y_sb, 1)
                if d_before:
                    act.wait_ge(comb_stored, 16 * j)
                act.wait_ge(cb_mm, j + 1)
                act.activation(cst[:, :], ps[:, 4, 0:TOK], ACT.Copy).then_inc(cb_sb, 1)
                act.wait_ge(yT_mm, j + 1)
                for k in range(2):
                    dst = yT[0:G, k].rearrange("x s (a p) -> x a s p", a=2)[:, :, :, j]
                    src = ps[0:G, 7, 128 * k:128 * k + 128].rearrange("x (a s) -> x a s", a=2)
                    act.activation(dst, src, ACT.Copy).then_inc(yT_sb, 1)

            def masked_queries(g, heads):
                for m in heads:
                    last = act.activation(qmh[:, g, m], qT[:, g], ACT.Identity, scale=mask[:, m:m + 1])
                last.then_inc(qmh_rdy, 1)
            phase1(act, step)

            def slot_step(u, n, v):
                act.wait_ge(fc1_mm, u + 1)
                act.activation(hg[:, :].rearrange("p (x f) -> p x f", x=2), ps[:, 0:2, 0:FH], ACT.Gelu)\
                    .then_inc(gelu_rdy, 1)
            phase2(act, slot_step)

            def out_step(p, n, w):
                act.wait_ge(nb3_rdy, p + 1)
                act.wait_ge(rstd3_rdy, p + 1)
                if not at_start(w):
                    act.wait_ge(out_stored[n], 16 * w)
                for t in range(4):
                    act.activation(o_sb[:, n, t], res[:, n, t], ACT.Identity,
                                   bias=nb3[:, n, t:t + 1], scale=rstd3[:, n, t:t + 1]).then_inc(o_rdy, 1)
                act.wait_ge(o_rdy, 4 * p + 4)
                act.dma_start(out_v[p], o_sb[:, n]).then_inc(out_stored[n], 16)
            phase3(act, out_step)

        @block.vector
        def _(dve):
            dve.memset(ident[:, :], 0.0).then_inc(ident_st, 1)
            dve.memset(mask[:, :], 1.0).then_inc(mask_st, 1)
            for n, e in enumerate((-0.5, 0.5, -1.0, EPS)):
                dve.memset(expo[:, n], e).then_inc(expo_st, 1)
            dve.memset(gst[:, :], 0.0).then_inc(gst_zeroed, 1)
            dve.memset(warm[:, :], 0.0).then_inc(zeroed, 1)
            dve.memset(vpad[:, :, :], 0.0).then_inc(zeroed, 1)
            dve.wait_ge(zeroed, 2)
            dve.tensor_copy(zs[:, :].rearrange("p (a n) -> p a n", a=2), vpad[0:ZK, 0:2, 0:TOK]).then_inc(zeroed, 1)
            dve.wait_ge(first_loaded, 16 * N_FIRST)
            dve.tensor_copy(wh[:, :, :], wst[:, :, :]).then_inc(w_split, 1)
            dve.wait_ge(w_split, 1)
            dve.tensor_tensor(wl[:, :, :], wst[:, :, :], wh[:, :, :].bitcast(F32), ALU.subtract).then_inc(w_split, 1)
            dve.wait_ge(loaded, 16 * N_LOADS)
            dve.tensor_copy(wqh[:, :, :], wqst[:, :, :]).then_inc(w_split, 1)
            dve.tensor_copy(wkh[:, :, :], wkst[:, :, :]).then_inc(w_split, 1)
            dve.tensor_copy(gw[:, :], gst[:, :]).then_inc(w_split, 1)
            dve.wait_ge(w_split, 5)
            dve.tensor_tensor(wql[:, :, :], wqst[:, :, :], wqh[:, :, :].bitcast(F32), ALU.subtract).then_inc(w_split, 1)
            dve.tensor_tensor(wkl[:, :, :], wkst[:, :, :], wkh[:, :, :].bitcast(F32), ALU.subtract).then_inc(w_split, 1)
            low = slice(ZT, ZK)
            dve.tensor_tensor(gw[low, :], gst[low, :], gw[low, :].bitcast(F32), ALU.subtract).then_inc(w_split, 1)
            dve.tensor_scalar(wo[0:G], wo[0:G], 0.5, None, ALU.mult).then_inc(wo_halved, 1)
            dve.tensor_tensor_reduce(out=slq[:, :], in0=sl[:, :], in1=sl[:, :], scale=1.0, scalar=0.0,
                                     op0=ALU.mult, op1=ALU.add, accum_out=slst[:, 0:1]).then_inc(sl_st, 1)
            dve.wait_ge(sl_st, 3)
            dve.reciprocal(slst[:, 2:3], slst[:, 1:2]).then_inc(sl_st, 1)
            dve.wait_ge(sl_st, 4)
            dve.tensor_scalar(slq[:, :], sl[:, :], slst[:, 2:3], slst[:, 3:4], ALU.mult, ALU.mult)\
                .then_inc(sl_st, 1)
            dve.wait_ge(slT_mm, 1)
            dve.tensor_copy(slT[:, :, :], ps[0:G, 7, 0:2 * S].rearrange("p (k s) -> p k s", k=2))\
                .then_inc(slT_sb, 1)
            dve.wait_ge(mask_st, 3)
            dve.wait_ge(dec_rdy, 1)
            dve.wait_ge(tables, 3)

            def statistics(j, x):
                dve.wait_ge(wo_mm, 2 * j + x + 1)
                for t in (2 * x, 2 * x + 1):
                    dve.bn_stats(st1[:, t, :], ps[0:T, 2 + x, (t % 2) * D:(t % 2) * D + D])

            def first_norm(j, x, d):
                statistics(j, x)
                dve.drain()
                for t in (2 * x, 2 * x + 1):
                    dve.bn_aggr(mv1[:, t, :], st1[:, t, :]).then_inc(mv1_rdy, 1)
                if d:
                    dve.wait_ge(tokT_mm, j)
                for t in (2 * x, 2 * x + 1):
                    dve.wait_ge(mv1_rdy, 4 * j + t + 1)
                    dve.scalar_tensor_tensor(t2[0:T, t], ps[0:T, 2 + x, (t % 2) * D:(t % 2) * D + D],
                                             mv1[:, t, 0:1], lnw[:, :], ALU.subtract, ALU.mult)\
                        .then_inc(t1_rdy, 1)

            def residual(j, x):
                dve.wait_ge(rstd1_rdy, 2 * j + x + 1)
                for t in (2 * x, 2 * x + 1):
                    dve.wait_ge(t1_rdy, 4 * j + t + 1)
                    dve.scalar_tensor_tensor(t2[0:T, t], t2[0:T, t], rstd1[:, t:t + 1], hb[0:T, t],
                                             ALU.mult, ALU.add).then_inc(t2_rdy, 1)

            def residual_statistics(j, x):
                for t in (2 * x, 2 * x + 1):
                    dve.wait_ge(t2_rdy, 4 * j + t + 1)
                    dve.bn_stats(st2[:, t, :], t2[0:T, t])
                dve.drain()
                for t in (2 * x, 2 * x + 1):
                    dve.bn_aggr(mv2[:, t, :], st2[:, t, :]).then_inc(mv2_rdy, 1)

            def second_norm(j):
                dve.wait_ge(mv2_rdy, 4 * j + 4)
                dve.wait_ge(rstd2_rdy, j + 1)
                if not (isinstance(j, int) and j == 0):
                    dve.wait_ge(h2_stored, 16 * j)
                for t in range(4):
                    dve.tensor_scalar(h2[0:T, t], t2[0:T, t], mv2[:, t, 0:1], rstd2[:, t:t + 1],
                                      ALU.subtract, ALU.mult).then_inc(h2_rdy, 1)

            def slot_tokens(j, d):
                dve.wait_ge(rr_rdy, j + 1)
                if d:
                    dve.wait_ge(y_mm, j)
                for t in range(4):
                    dve.wait_ge(h2_rdy, 4 * j + t + 1)
                    dve.scalar_tensor_tensor(xn[0:T, t], h2[0:T, t], rr[:, t:t + 1], nw[:, :],
                                             ALU.mult, ALU.mult).then_inc(xn_rdy, 1)
                for t in range(4):
                    dve.wait_ge(xn_rdy, 4 * j + t + 1)
                    dve.tensor_tensor_reduce(out=tok[0:T, t], in0=xn[0:T, t], in1=xn[0:T, t], scale=1.0,
                                             scalar=0.0, op0=ALU.mult, op1=ALU.add,
                                             accum_out=ss[:, t:t + 1]).then_inc(ss_rdy, 1)
                dve.wait_ge(ss_rdy, 4 * j + 4)
                dve.tensor_scalar(nrm[:, :], ss[:, :], EPS * EPS, None, ALU.max).then_inc(nrm_rdy, 1)

            def decay(i, k, units=range(UNITS)):
                g, a = ORDER[k]
                if k >= 2:
                    dve.wait_ge(pv_mm, 4 * i + k - 1)
                for u in units:
                    h0 = UNIT[u][0]
                    dve.wait_ge(sc_mm, 4 * UNITS * i + UNITS * k + u + 1)
                    src = ps[0:T, 2 + (UNITS * k + u) % SC_BANKS, 0:UH * T].rearrange("p (h n) -> p h n", h=UH)
                    dst = p_sb[:, k % 2, u].rearrange("p (h n) -> p h n", h=UH)
                    dve.tensor_tensor(dst, src, dec[:, g * HG + h0:g * HG + h0 + UH], ALU.mult).then_inc(p_rdy, 1)

            def early_queries(i, g):
                dve.wait_ge(qh_rdy, 2 * i + g + 1)
                for m in range(EARLY[g]):
                    last = dve.tensor_scalar(qmh[:, g, m], qh[:, g].bitcast(F32), mask[:, m:m + 1], None, ALU.mult)
                last.then_inc(dqmh_rdy, 1)

            def masked_queries(g, heads):
                for m in heads:
                    last = dve.tensor_scalar(qml[:, g, m], ql[:, g], mask[:, m:m + 1], None, ALU.mult)
                last.then_inc(qml_rdy, 1)

            def gated(i, g):
                dve.wait_ge(pv_mm, 4 * i + 2 * g + 2)
                dve.wait_ge(g_sb, 2 * i + g + 1)
                dve.scalar_tensor_tensor(og[:, g], gt[:, g], 1.0, ps[0:G, 5 + g, 0:PT],
                                         ALU.add, ALU.mult).then_inc(og_sb, 1)

            def maxima(j):
                dve.wait_ge(Ls_rdy, j + 1)
                dve.reduce_max(lmx[:, :], Ls[:, :], AX).then_inc(lmx_rdy, 1)
                dve.wait_ge(lt_mm, j + 1)
                lt = ps[0:T, 7, 256:512].rearrange("p (x s) -> p x s", s=S)
                dve.reduce_max(cmx[:, :], lt, AX).then_inc(cmx_rdy, 1)
                dve.wait_ge(cmx_rdy, j + 1)
                dve.tensor_tensor(Lc[:, :, :], lt, cmx[:, :].unsqueeze(2).to_broadcast([T, 4, S]),
                                  ALU.subtract).then_inc(Lc_rdy, 1)

            def sums(j):
                dve.wait_ge(Es_rdy, j + 1)
                dve.reciprocal(lrec[:, :], lsum[:, :]).then_inc(lrec_rdy, 1)
                dve.wait_ge(Ec_rdy, j + 1)
                dve.reduce_sum(csum[:, :], Ec[:, :, :], AX).then_inc(csum_rdy, 1)
                dve.wait_ge(csum_rdy, j + 1)
                dve.reciprocal(crec[:, :], csum[:, :]).then_inc(crec_rdy, 1)

            def low_h(i, g):
                dve.wait_ge(hTh_rdy, 2 * i + g + 1)
                dve.tensor_tensor(hTl[:, g], hT[:, g], hTh[:, g].bitcast(F32), ALU.subtract).then_inc(hTl_rdy, 1)

            def step(i, a, c, d, d_before, more):
                if d and not (a or c):
                    maxima(i - 2)
                    sums(i - 2)
                if a:
                    low_h(i, 0)
                if c:
                    first_norm(i - 1, 0, d)
                    if not a:
                        first_norm(i - 1, 1, d)
                        maxima(i - 2)
                    residual(i - 1, 0)
                    if not a:
                        residual(i - 1, 1)
                        sums(i - 2)
                    residual_statistics(i - 1, 0)
                    if not a:
                        residual_statistics(i - 1, 1)
                if a:
                    low_h(i, 1)
                    if c:
                        first_norm(i - 1, 1, d)
                    dve.wait_ge(q_mm, 2 * i + 2)
                    dve.tensor_copy(zt[:, :], ps[G:G + RANK, 1, 0:PT]).then_inc(z_sb, 1)
                    if c:
                        residual(i - 1, 1)
                    early_queries(i, 0)
                    dve.wait_ge(ql_rdy, 2 * i + 1)
                    masked_queries(0, range(HG))
                    if c:
                        dve.wait_ge(t2_rdy, 4 * i)
                    dve.wait_ge(ht_mm, i + 1)
                    dve.tensor_tensor(hb[:, :, :].rearrange("p (x t) d -> p x t d", x=2),
                                      ps[0:T, 5:7, 0:2 * D].rearrange("p x (t d) -> p x t d", t=2),
                                      lnb[:, :].unsqueeze(1).unsqueeze(1).to_broadcast([T, 2, 2, D]), ALU.add)\
                        .then_inc(hb_sb, 1)
                    decay(i, 0, range(2))
                    early_queries(i, 1)
                    dve.wait_ge(kt_mm, i + 1)
                    dve.tensor_tensor(kts[:, :, :].rearrange("p a (h d) -> p a h d", h=H),
                                      ps[0:T, 5, 0:2 * D].rearrange("p (a h d) -> p a h d", a=2, h=H),
                                      kdec[:, :].unsqueeze(1).unsqueeze(3).to_broadcast([T, 2, H, HD]),
                                      ALU.mult).then_inc(kts_rdy, 1)
                    dve.wait_ge(ql_rdy, 2 * i + 2)
                    masked_queries(1, range(LOW))
                    decay(i, 0, range(2, UNITS))
                    decay(i, 1, range(2))
                    dve.wait_ge(s_mm, i + 1)
                    dve.tensor_tensor(state[:, :, :].rearrange("p x (h d) -> p x h d", h=HG),
                                      ps[0:G, 6, 0:4 * G].rearrange("p (x h d) -> p x h d", x=4, h=HG),
                                      mask[:, :].unsqueeze(1).unsqueeze(3).to_broadcast([G, 4, HG, HD]),
                                      ALU.mult).then_inc(s_sb, 1)
                    if c:
                        residual_statistics(i - 1, 1)
                    decay(i, 1, range(2, UNITS))
                if d and a:
                    maxima(i - 2)
                if a:
                    decay(i, 2)
                if d and a:
                    sums(i - 2)
                if c:
                    second_norm(i - 1)
                if a:
                    decay(i, 3)
                    gated(i, 0)
                if c:
                    slot_tokens(i - 1, d)
                if a:
                    gated(i, 1)
            phase1(dve, step)

            dve.wait_ge(yT_mm, NP)
            dve.memset(ybuf[G:G + 1, :, :, :, :], 1.0).then_inc(ones_rdy, 1)

            def slot_step(u, n, v):
                par = n % 2
                dve.wait_ge(tr_mm, u + 1)
                dve.tensor_copy(hgT[:, :, :].rearrange("p (x j) b -> p x (j b)", x=2), ps[:, 2:4, 0:FH])\
                    .then_inc(hgT_rdy, 1)
                if not (isinstance(u, int) and u < 2):
                    dve.wait_ge(y2_stored[par], 16 * (RING // 2 * v + n // 2))
                dve.wait_ge(fc2_mm, u + 1)
                dve.tensor_copy(y2st[:, par], ps[:, 4 + par, 0:D]).then_inc(y2st_rdy, 1)
            phase2(dve, slot_step)

            def out_step(p, n, w):
                dve.wait_ge(cmb_mm, p + 1)
                dve.wait_ge(h2r_loaded[n], 16 * w + 16)
                if not at_start(w):
                    dve.wait_ge(o_rdy, 4 * (p + 1 - DEEP))
                dve.tensor_tensor(res[0:T, n].rearrange("p (x t) d -> p x (t d)", x=2),
                                  ps[0:T, 2 * n:2 * n + 2, 0:2 * D],
                                  h2r[:, n].rearrange("p (x t) d -> p x (t d)", x=2), ALU.add)\
                    .then_inc(res_rdy, 1)
                dve.wait_ge(res_rdy, p + 1)
                for t in range(4):
                    dve.bn_stats(st3[:, n, t, :], res[0:T, n, t])
                dve.drain()
                for t in range(4):
                    dve.bn_aggr(mv3[:, n, t, :], st3[:, n, t, :]).then_inc(mv3_rdy, 1)
                if not (at_start(w) and n == 0):
                    shift(p - 1, (n - 1) % DEEP)

            def shift(p, n):
                dve.wait_ge(rstd3_rdy, p + 1)
                dve.scalar_tensor_tensor(nb3[:, n], mv3[:, n, :, 0], -1.0, rstd3[:, n],
                                         ALU.mult, ALU.mult).then_inc(nb3_rdy, 1)
            phase3(dve, out_step)
            shift(NP - 1, DEEP - 1)

        @block.tensor
        def _(pe):
            pe.wait_ge(w_split, 2)

            def product(out, hi, lo, x_hi, x_lo, start, stop):
                pe.matmul(out, hi, x_lo, start=start, stop=False)
                pe.matmul(out, lo, x_hi, start=False, stop=False)
                return pe.matmul(out, hi, x_hi, start=False, stop=stop)

            def project(i, g, hi, lo, done, more=0):
                for k in range(2):
                    pe.wait_ge(hTl_rdy, 2 * i + k + 1)
                    c = slice(g * G, (g + 1) * G + more)
                    mm = product(ps[0:G + more, g, 0:PT], hi[:, k, c], lo[:, k, c], hTh[:, k], hTl[:, k],
                                 k == 0, k == 1)
                mm.then_inc(done, 1)

            def gate(i):
                pe.wait_ge(k_sb, 2 * i + 2)
                pe.wait_ge(zh_rdy, 2 * i + 2)
                pe.wait_ge(zl_rdy, i + 1)
                for g in range(2):
                    pe.matmul(ps[0:G, g, 0:PT], gw[:, g * G:(g + 1) * G], zs[:, :], start=True, stop=True)\
                        .then_inc(g_mm, 1)

            def slots_turned():
                pe.wait_ge(ident_st, 2)
                pe.wait_ge(sl_st, 5)
                for k in range(2):
                    mm = pe.transpose(ps[0:G, 7, k * S:(k + 1) * S], slq[:, k * G:(k + 1) * G], ident[0:S, 0:S])
                mm.then_inc(slT_mm, 1)

            def project_out(j, x):
                pe.wait_ge(og_sb, 2 * j + 2)
                for t in (2 * x, 2 * x + 1):
                    for k in range(2):
                        mm = pe.matmul(ps[0:T, 2 + x, (t % 2) * D:(t % 2) * D + D],
                                       og[0:G, k, t * T:(t + 1) * T], wo[0:G, k], start=(k == 0), stop=(k == 1))
                mm.then_inc(wo_mm, 1)

            def embed(i, g, c):
                if c:
                    pe.wait_ge(g_sb, 2 * i - 1 + g)
                for k in range(KP):
                    if g == 0:
                        pe.wait_ge(xl_rdy, KP * i + k + 1)
                    c = slice(g * G, (g + 1) * G)
                    mm = product(ps[0:G, g, 0:PT], wh[:, k, c], wl[:, k, c], xh[:, k], xl[:, k],
                                 k == 0, k == KP - 1)
                mm.then_inc(hT_mm, 1)

            def scores(i, k, c):
                g, a = ORDER[k]
                if k % 2 == 0:
                    pe.wait_ge(kl_rdy, 2 * i + g + 1)
                    pe.wait_ge(qmh_rdy, 2 * i + g + 1)
                    pe.wait_ge(dqmh_rdy, 2 * i + g + 1)
                    if g == 1:
                        pe.wait_ge(qml1_rdy, (HG - LOW) * (i + 1))
                    pe.wait_ge(qml_rdy, 2 * i + g + 1)
                for u, (h0, mt) in enumerate(UNIT):
                    unit = UNITS * k + u
                    if unit >= SC_BANKS:
                        pe.wait_ge(p_rdy, 4 * UNITS * i + unit - SC_BANKS + 1)
                    elif unit < 2:
                        if c:
                            pe.wait_ge(t1_rdy, 4 * i)
                    else:
                        pe.wait_ge(v_sb, 2 * i + 1)
                    n = slice(a * TOK + mt * T, a * TOK + mt * T + T)
                    h = slice(h0, h0 + UH)
                    product(ps[0:T, 2 + unit % SC_BANKS, 0:UH * T].rearrange("p (h n) -> p h n", h=UH),
                            kh[:, g, n], kl[:, g, n], qmh[:, g, h, n], qml[:, g, h, n],
                            True, True).then_inc(sc_mm, 1)

            def keys_turned(i):
                pe.wait_ge(k_sb, 2 * i + 2)
                pe.wait_ge(hb_sb, i + 1)
                for a in range(2):
                    for g in range(2):
                        mm = pe.transpose(ps[0:T, 5, a * D + g * G:a * D + (g + 1) * G],
                                          kT[:, g, a * TOK:a * TOK + T], ident[0:G, 0:G])
                mm.then_inc(kt_mm, 1)

            def states(i):
                pe.wait_ge(kts_rdy, i + 1)
                pe.wait_ge(v_sb, 2 * i + 2)
                for g, a in ORDER:
                    v = vpad[:, 2 * a].rearrange("p (j q d) -> p j q d", q=4, d=HD)
                    mm = pe.matmul(ps[0:G, 6, (2 * g + a) * G:(2 * g + a + 1) * G]
                                   .rearrange("p (j q d) -> p j q d", q=2, d=HD),
                                   kts[:, a, g * G:(g + 1) * G], v[:, 3 * g:3 * g + 3, 0:4:3, :],
                                   start=True, stop=True)
                mm.then_inc(s_mm, 1)

            def values(i, k):
                g, a = ORDER[k]
                pe.wait_ge(s_sb, i + 1)
                pe.wait_ge(qd_rdy, 2 * i + g + 1)
                pe.wait_ge(p_rdy, 4 * UNITS * i + UNITS * (k + 1))
                for mt in range(2):
                    out = [ps[32 * b:32 * b + 32, 5 + g, a * TOK + mt * T:a * TOK + mt * T + T]
                           for b in range(HG // 2)]
                    for odd in range(2):
                        for b in range(HG // 2):
                            h = 2 * b + odd
                            mm = pe.matmul(out[b], vpad[:, 2 * a + mt, 32 * (g * HG + h):32 * (g * HG + h) + 32],
                                           p_sb[:, k % 2, 2 * mt + h // UH, (h % UH) * T:(h % UH + 1) * T],
                                           start=(odd == 0), stop=(odd == 1 and mt == 0))
                    if mt == 1:
                        for b in range(HG // 2):
                            mm = pe.matmul(out[b], state[:, 2 * g + a, 32 * b:32 * b + 32], qd[:, g, a],
                                           start=False, stop=True)
                mm.then_inc(pv_mm, 1)

            def slot_inputs_turned(j):
                pe.wait_ge(y_sb, j + 1)
                for k in range(2):
                    mm = pe.transpose(ps[0:G, 7, 128 * k:128 * k + 128], ysb[:, k * G:(k + 1) * G], ident[:, :])
                mm.then_inc(yT_mm, 1)

            def combine_turned(j):
                pe.wait_ge(Cn_rdy, j + 1)
                for k in range(2):
                    mm = pe.transpose(ps[:, 4, k * T:(k + 1) * T], Cn[:, 2 * k:2 * k + 2, :], ident[0:T, 0:T])
                mm.then_inc(cb_mm, 1)

            def token_features(j):
                for t in range(4):
                    pe.wait_ge(tok_rdy, 4 * j + t + 1)
                    for k in range(2):
                        mm = pe.transpose(ps[0:G, 5 + k, t * T:(t + 1) * T], tok[0:T, t, k * G:(k + 1) * G],
                                          ident[0:T, 0:T])
                mm.then_inc(tokT_mm, 1)

            def logits(j):
                pe.wait_ge(tokT_sb, j + 1)
                for k in range(2):
                    for a in range(2):
                        mm = pe.matmul(ps[64 * a:64 * a + 64, 7, 0:TOK], slT[:, k, :],
                                       tokT[0:G, k, a * TOK:(a + 1) * TOK], start=(k == 0), stop=(k == 1))
                mm.then_inc(lg_mm, 1)

            def logits_turned(j):
                pe.wait_ge(Ls_rdy, j + 1)
                for k in range(2):
                    mm = pe.transpose(ps[0:T, 7, 256 + 128 * k:256 + 128 * k + 128], Ls[:, k * T:(k + 1) * T], ident[:, :])
                mm.then_inc(lt_mm, 1)

            def dispatch_turned(j):
                pe.wait_ge(Dn_rdy, j + 1)
                for k in range(2):
                    mm = pe.transpose(ps[0:T, 1, 128 * k:128 * k + 128], Dn[:, k * T:(k + 1) * T], ident[:, :])
                mm.then_inc(dt_mm, 1)

            def slot_inputs(j):
                pe.wait_ge(Lc_rdy, j + 1)
                pe.wait_ge(DT_sb, j + 1)
                for k in range(2):
                    for a in range(2):
                        mm = pe.matmul(ps[64 * a:64 * a + 64, 7, 0:D], DT[:, k, 64 * a:64 * a + 64],
                                       xn[0:T, 2 * a + k], start=(k == 0), stop=(k == 1))
                mm.then_inc(y_mm, 1)

            def step(i, a, c, d, d_before, more):
                if a:
                    embed(i, 0, c)
                if c:
                    project_out(i - 1, 0)
                    if not a:
                        project_out(i - 1, 1)
                if d:
                    if c:
                        pe.wait_ge(og_sb, 2 * i)
                    token_features(i - 2)
                if a:
                    embed(i, 1, c)
                if a:
                    if c:
                        project_out(i - 1, 1)
                    if d:
                        pe.wait_ge(tokT_sb, i - 1)
                    for k in range(2):
                        pe.wait_ge(hT_sb, 2 * i + k + 1)
                        for t in range(4):
                            mm = pe.transpose(ps[0:T, 5 + t // 2, (t % 2) * D + k * G:(t % 2) * D + (k + 1) * G],
                                              hT[:, k, t * T:(t + 1) * T], ident[0:G, 0:G])
                    mm.then_inc(ht_mm, 1)
                    if at_start(i):
                        pe.wait_ge(loaded, 16 * N_LOADS)
                        pe.wait_ge(w_split, 8)
                        pe.wait_ge(wo_halved, 1)
                        slots_turned()
                    project(i, 0, wqh, wql, q_mm)
                    project(i, 1, wqh, wql, q_mm, more=RANK)
                    for g in range(2):
                        pe.wait_ge(q_sb, 2 * i + g + 1)
                        if g == 1:
                            pe.wait_ge(z_sb, i + 1)
                        project(i, g, wkh, wkl, k_mm)
                    for t in range(4):
                        if t == 0 and d_before:
                            pe.wait_ge(cb_sb, i - 2)
                        if t == 2 and at_start(i):
                            pe.wait_ge(slT_sb, 1)
                        if t == 2 and d_before:
                            pe.wait_ge(yT_sb, 2 * i - 4)
                        for k in range(2):
                            mm = pe.matmul(ps[0:T, 4 + 3 * (t // 2), (t % 2) * D:(t % 2) * D + D],
                                           hT[:, k, t * T:(t + 1) * T], wv[:, k], start=(k == 0), stop=(k == 1))
                        if t % 2:
                            mm.then_inc(v_mm, 1)
                    scores(i, 0, c)
                    keys_turned(i)
                if d:
                    if a:
                        pe.wait_ge(v_sb, 2 * i + 2)
                    else:
                        pe.wait_ge(yT_sb, 2 * i - 4)
                    logits(i - 2)
                if a:
                    states(i)
                    scores(i, 1, c)
                if d:
                    logits_turned(i - 2)
                if a:
                    gate(i)
                    values(i, 0)
                    scores(i, 2, c)
                    values(i, 1)
                if d:
                    if a:
                        pe.wait_ge(g_sb, 2 * i + 2)
                    dispatch_turned(i - 2)
                if a:
                    scores(i, 3, c)
                    values(i, 2)
                if d:
                    slot_inputs(i - 2)
                if a:
                    values(i, 3)
                if d:
                    if not a:
                        pe.wait_ge(cb_sb, i - 2)
                    combine_turned(i - 2)
                    slot_inputs_turned(i - 2)
            phase1(pe, step)
            pe.wait_ge(cb_sb, NP)
            pe.wait_ge(ones_rdy, 1)

            def fc2_pair(u, n):
                pe.wait_ge(hgT_rdy, u + 1)
                if not (isinstance(u, int) and u < 2):
                    pe.wait_ge(y2st_rdy, u - 1)
                for k in range(FJ):
                    for s in range(2):
                        mm = pe.matmul(ps[64 * s:64 * s + 64, 4 + n % 2, 0:D], hgT[:, k, 64 * s:64 * s + 64],
                                       w2v[n][:, s, k], start=(k == 0), stop=(k == FJ - 1))
                mm.then_inc(fc2_mm, 1)

            def slot_step(u, n, v):
                start = isinstance(u, int) and u == 0
                pe.wait_ge(w_loaded[n], 32 * v + 32)
                pe.wait_ge(ybuf_rdy, u + 1)
                if not start:
                    pe.wait_ge(gelu_rdy, u)
                for x in range(2):
                    for k in range(2):
                        for s in range(2):
                            mm = pe.matmul(ps[64 * s:64 * s + 64, x, 0:FH], ybuf[0:G + k, n % 2, k, s],
                                           w1v[n][0:G + k, s, k, x * FH:(x + 1) * FH],
                                           start=(k == 0), stop=(k == 1))
                mm.then_inc(fc1_mm, 1)
                if not start:
                    fc2_pair(u - 1, (n - 1) % RING)
                pe.wait_ge(gelu_rdy, u + 1)
                if not start:
                    pe.wait_ge(hgT_rdy, u)
                for k in range(FJ):
                    mm = pe.transpose(ps[:, 2 + k // 3, (k % 3) * 128:(k % 3) * 128 + 128],
                                      hg[:, 128 * k:128 * k + 128], ident[:, :])
                mm.then_inc(tr_mm, 1)
            phase2(pe, slot_step)
            fc2_pair(NU - 1, (NU - 1) % RING)

            pe.wait_ge(hgT_rdy, NU)
            def out_step(p, n, w):
                pe.wait_ge(cbuf_loaded[n], 16 * w + 16)
                pe.wait_ge(y2b_rdy, p + 1)
                if not at_start(w):
                    pe.wait_ge(res_rdy, p + 1 - DEEP)
                for t in range(4):
                    a, k = t // 2, t % 2
                    mm = pe.matmul(ps[0:T, 2 * n + a, k * D:(k + 1) * D],
                                   cbuf[64 * a:64 * a + 64, n, k * T:(k + 1) * T],
                                   y2b[64 * a:64 * a + 64, n, :], start=True, stop=True)
                mm.then_inc(cmb_mm, 1)
            phase3(pe, out_step)


N_FIRST, N_LOADS = 3, 15


def kernel(**inputs):
    import numpy as np
    import concourse.bacc as bacc
    from concourse.bass_utils import run_bass_kernel_spmd

    g = {k: np.asarray(v) for k, v in inputs.items()}
    x = g["x"].reshape(NP, 2, C_IN, GRID, PATCH, GRID, PATCH).transpose(0, 4, 6, 2, 1, 3, 5)
    arrays = {
        "xT": x.reshape(NP, KP, 128, PT).transpose(0, 2, 1, 3),
        "W": g["L0_tok_W"].T.reshape(KP, 128, D).transpose(1, 0, 2),
        "Wq": g["L0_attn_Wq"].reshape(2, G, D).transpose(1, 0, 2),
        "Wk": g["L0_attn_Wk"].reshape(2, G, D).transpose(1, 0, 2),
        "Wv": g["L0_attn_Wv"].reshape(2, G, D).transpose(1, 0, 2),
        "Wo": g["L0_attn_Wo"].reshape(2, G, D).transpose(1, 0, 2),
        "Wg1": g["L0_attn_Wg1"].reshape(2, G, RANK).transpose(1, 0, 2),
        "Wg2": g["L0_attn_Wg2"],
        "log_slope": g["L0_attn_log_slope"],
        "row_slope": np.repeat(g["L0_attn_log_slope"], HD).reshape(2, G).T,
        "ln_w": g["L0_attn_ln_w"],
        "ln_b": g["L0_attn_ln_b"],
        "slots": g["L0_ffn_slots"],
        "scale": g["L0_ffn_scale"].reshape(S, 1),
        "fc1": np.concatenate([
            g["L0_ffn_fc1_weight"].reshape(NU, 2, 2, G, F).transpose(0, 3, 1, 2, 4),
            np.stack([np.zeros((NU, 1, 2, F), np.float32), g["L0_ffn_fc1_bias"].reshape(NU, 1, 2, F)], axis=3),
        ], axis=1),
        "fc2": g["L0_ffn_fc2_weight"].reshape(NU, 2, FJ, 128, D).transpose(0, 3, 1, 2, 4),
        "fc2b": g["L0_ffn_fc2_bias"],
        "norm_w": g["L0_ffn_norm_weight"],
    }
    nc = bacc.Bacc("TRN2", target_bir_lowering=False, num_devices=1)
    feed, aps = {}, []
    for name, a in arrays.items():
        feed[f"in_{name}"] = np.ascontiguousarray(a)
        aps.append(nc.dram_tensor(f"in_{name}", list(a.shape), F32, kind="ExternalInput").ap())
    out = nc.dram_tensor("out", [NB, TOK, D], F32, kind="ExternalOutput").ap()
    vit_tower(nc, *aps, out)
    r = run_bass_kernel_spmd(nc, [feed], core_ids=[0])
    return r.results[0]["out"]
```
